# Optimizing a Trainium2 kernel written in Bass

```python
import numpy as np
import jax
import jax.numpy as jnp

def _softmax(x, axis=-1):
    return jax.nn.softmax(x, axis=axis)

def _gelu(x):
    return jax.nn.gelu(x, approximate=True)

def _silu(x):
    return jax.nn.silu(x)

def _sigmoid(x):
    return jax.nn.sigmoid(x)

def _layernorm(x, axis=-1, eps=1e-05):
    m = jnp.mean(x, axis=axis, keepdims=True)
    v = jnp.var(x, axis=axis, keepdims=True)
    return (x - m) / jnp.sqrt(v + eps)

def _scatter_add(tgt, idx, src, axis=0):
    return tgt.at[idx].add(src)

def _segment_sum(src, seg, n):
    return jax.ops.segment_sum(src, seg, n)
kernel_name = 'mk_decoder_preln_d2_seqx_r8_f68a12'

def setup_inputs(seed: int=0):
    np.random.seed(seed)
    _w = jnp.asarray

    def _rec_inputs():
        import jax
        import jax.numpy as jnp
        _rk = jax.random.key(seed)
        x = 7.22e-05 + 1 * jax.random.normal(jax.random.fold_in(_rk, 1), (32, 64, 256), jnp.float32)
        _lenS = 64 - jax.random.randint(jax.random.fold_in(_rk, 7), (32,), 0, max(1, 64 // 4) + 1, jnp.int32)
        _lenS2 = 64 - jax.random.randint(jax.random.fold_in(_rk, 8), (32,), 0, max(1, 64 // 4) + 1, jnp.int32)
        _ctx_512P = jax.random.normal(jax.random.fold_in(_rk, 11), (32, 16, 64), jnp.float32)
        _ctx_512c = jax.random.dirichlet(jax.random.fold_in(_rk, 511), 0.3 * jnp.ones((16,), jnp.float32), (32, 64))
        _ctx_512t = jnp.einsum('bsk,bkd->bsd', _ctx_512c, _ctx_512P)
        _ctx_512t = _ctx_512t * jax.lax.rsqrt(jnp.mean(jnp.square(_ctx_512t)) + 1e-12) * 0.953939
        ctx_512 = -0.000514642 + 1.00011 * (_ctx_512t + 0.3 * jax.random.normal(jax.random.fold_in(_rk, 611), (32, 64, 64), jnp.float32))
        return (x, ctx_512)
    x, ctx_512 = _rec_inputs()

    def _L0_attn_setup():
        import jax, jax.numpy as jnp
        import numpy as np
        BATCH, SEQ, D_MODEL, N_HEADS, D_HEAD = (2, 256, 256, 16, 128)
        ATTN_SCALE = np.sqrt(D_HEAD).astype(np.float32)
        IGNORE = jnp.float32(-100000.0)
        key = jax.random.key(seed)
        ks = jax.random.split(key, 5)
        init = 1.0 / np.sqrt(D_MODEL)
        return {'x': jax.random.normal(ks[0], (BATCH, SEQ, D_MODEL), jnp.float32), 'W_Q': jax.random.normal(ks[1], (N_HEADS, D_MODEL, D_HEAD), jnp.float32) * init, 'W_K': jax.random.normal(ks[2], (N_HEADS, D_MODEL, D_HEAD), jnp.float32) * init, 'W_V': jax.random.normal(ks[3], (N_HEADS, D_MODEL, D_HEAD), jnp.float32) * init, 'W_O': jax.random.normal(ks[4], (N_HEADS, D_HEAD, D_MODEL), jnp.float32) * init, 'b_Q': jnp.zeros((N_HEADS, D_HEAD), jnp.float32), 'b_K': jnp.zeros((N_HEADS, D_HEAD), jnp.float32), 'b_V': jnp.zeros((N_HEADS, D_HEAD), jnp.float32), 'b_O': jnp.zeros((D_MODEL,), jnp.float32)}
    _L0_attn_all = _L0_attn_setup()
    _L0_attn_in = {k: v for k, v in _L0_attn_all.items() if k in ('W_Q', 'W_K', 'W_V', 'W_O', 'b_Q', 'b_K', 'b_V', 'b_O')}
    del _L0_attn_all

    def _L0_xattn_setup():
        import jax, jax.numpy as jnp
        import numpy as np
        import math
        NUM_Q_HEADS = 32
        NUM_KV_HEADS = 8
        key = jax.random.key(seed)
        k1, k2, k3 = jax.random.split(key, 3)
        B, S, E = (2, 256, 256)
        kv_E = NUM_KV_HEADS * (E // NUM_Q_HEADS)
        q = jax.random.normal(k1, (B, S, E), dtype=jnp.float32)
        k = jax.random.normal(k2, (B, S, kv_E), dtype=jnp.float32)
        v = jax.random.normal(k3, (B, S, kv_E), dtype=jnp.float32)
        return {'q': q, 'k': k, 'v': v}
    _L0_xattn_all = _L0_xattn_setup()
    _L0_xattn_in = {k: v for k, v in _L0_xattn_all.items() if k in ()}
    del _L0_xattn_all

    def _L0_ffn_setup():
        import jax, jax.numpy as jnp
        import numpy as np
        B_, S, D = (2, 256, 256)
        F_ = 1024
        R = 16
        H = 16
        HD = D // H
        MOD_SCALE = 0.1
        EPS = 1e-06

        def _rmsnorm(x, w):
            v = jnp.mean(x * x, axis=-1, keepdims=True)
            return x * jax.lax.rsqrt(v + EPS) * w

        def _attention(x, Wq, Wk, Wv, Wo):
            b, s, d = x.shape
            q = (x @ Wq.T).reshape(b, s, H, HD)
            k = (x @ Wk.T).reshape(b, s, H, HD)
            v = (x @ Wv.T).reshape(b, s, H, HD)
            scores = jnp.einsum('bqhd,bkhd->bhqk', q, k) / np.sqrt(HD).astype(np.float32)
            causal = jnp.tril(jnp.ones((s, s), bool))
            scores = jnp.where(causal, scores, jnp.finfo(scores.dtype).min)
            probs = jax.nn.softmax(scores, axis=-1)
            out = jnp.einsum('bhqk,bkhd->bqhd', probs, v).reshape(b, s, d)
            return out @ Wo.T
        key = jax.random.key(seed)
        ks = jax.random.split(key, 12)
        sd = 0.02
        return {'hidden_states': jax.random.normal(ks[0], (B_, S, D), jnp.float32), 'ln1_w': jnp.ones((D,), jnp.float32), 'ln2_w': jnp.ones((D,), jnp.float32), 'Wq': jax.random.normal(ks[1], (D, D), jnp.float32) * sd, 'Wk': jax.random.normal(ks[2], (D, D), jnp.float32) * sd, 'Wv': jax.random.normal(ks[3], (D, D), jnp.float32) * sd, 'Wo': jax.random.normal(ks[4], (D, D), jnp.float32) * sd, 'A': jax.random.normal(ks[5], (D, R), jnp.float32) * (0.01 / np.sqrt(D)), 'B': jax.random.normal(ks[6], (R, F_), jnp.float32) * (0.01 / np.sqrt(R)), 'W_in_base': jax.random.normal(ks[7], (F_, D), jnp.float32) * sd, 'W_up_base': jax.random.normal(ks[8], (F_, D), jnp.float32) * sd, 'W_down': jax.random.normal(ks[9], (D, F_), jnp.float32) * sd}
    _L0_ffn_all = _L0_ffn_setup()
    _L0_ffn_in = {k: v for k, v in _L0_ffn_all.items() if k in ('ln1_w', 'ln2_w', 'Wq', 'Wk', 'Wv', 'Wo', 'A', 'B', 'W_in_base', 'W_up_base', 'W_down')}
    del _L0_ffn_all

    def _L1_attn_setup():
        import jax, jax.numpy as jnp
        import numpy as np
        from jax import lax
        B, L, D = (2, 512, 256)
        K, KQ, M, H = (32, 4, 8, 8)
        MEM = K * H
        FLAT = K * H * M
        CONV_W = 4
        DIM_SWIGLU = H * 3 * 2
        N_DECAY = K - 4

        def _forward(x, W_mem, conv_k, W_q, theta, decay_slopes, anchor_slopes, score_scale, W_re, W_im, norm_scale, W_out):
            b, l, d = x.shape
            z = x @ W_mem
            z = lax.conv_general_dilated(z, conv_k, window_strides=(1,), padding=[(CONV_W - 1, 0)], dimension_numbers=('NHC', 'HIO', 'NHC'), feature_group_count=MEM + K)
            k_val = z[..., :MEM].reshape(b, l, K, H)
            s_raw = z[..., MEM:].reshape(b, l, K, 1)
            q = (x @ W_q).reshape(b, l, KQ, H, M, 2)
            q_re, q_im = (q[..., 0], q[..., 1])
            pos = jnp.arange(l, dtype=jnp.float32)
            slopes_d = jax.nn.softplus(decay_slopes).reshape(1, 1, -1, 1)
            slopes_a = jax.nn.softplus(anchor_slopes).reshape(1, 1, -1, 1)
            dist = jnp.maximum(jnp.float32(l - 1) - pos, 0.0)
            log_w = jnp.concatenate([-slopes_d * dist[None, :, None, None], -slopes_a * pos[None, :, None, None]], axis=2)
            log_p = jnp.clip(score_scale[None, None, :, None] * s_raw, -20.0, 20.0)
            p_w = jnp.exp(log_p + log_w)
            phi = k_val[..., None] * theta
            re_k, im_k = (jnp.cos(phi), jnp.sin(phi))
            pw5 = p_w[..., None]
            merged = jnp.concatenate([p_w.squeeze(-1), (pw5 * re_k).reshape(b, l, FLAT), (pw5 * im_k).reshape(b, l, FLAT)], axis=-1)
            cs = jnp.cumsum(merged, axis=1)
            den = cs[..., :K]
            num_re = cs[..., K:K + FLAT]
            num_im = cs[..., K + FLAT:]
            inv_den = 1.0 / jnp.maximum(den[..., None], 0.0001)
            state_re = num_re.reshape(b, l, K, H, M) * inv_den[..., None]
            state_im = num_im.reshape(b, l, K, H, M) * inv_den[..., None]
            n_rep = K // KQ
            q_re = jnp.repeat(q_re, n_rep, axis=2)
            q_im = jnp.repeat(q_im, n_rep, axis=2)
            out_re = jnp.sum(state_re * q_re + state_im * q_im, axis=-1)
            out_im = jnp.sum(state_im * q_re - state_re * q_im, axis=-1)
            out_re = out_re * norm_scale
            out_im = out_im * norm_scale
            y = jnp.einsum('blkh,khn->blkn', out_re, W_re) + jnp.einsum('blkh,khn->blkn', out_im, W_im)
            y_val, y_gate = jnp.split(y, 2, axis=-1)
            y = (y_val * jax.nn.silu(y_gate)).reshape(b, l, -1)
            return y @ W_out
        key = jax.random.key(seed)
        ks = jax.random.split(key, 8)
        x = jax.random.normal(ks[0], (B, L, D), dtype=jnp.float32)
        W_mem = jax.random.normal(ks[1], (D, MEM + K), dtype=jnp.float32) / np.sqrt(D)
        conv_k = jax.random.normal(ks[2], (CONV_W, 1, MEM + K), dtype=jnp.float32) * 0.3
        W_q = jax.random.normal(ks[3], (D, KQ * H * M * 2), dtype=jnp.float32) / np.sqrt(D)
        theta = jnp.asarray(np.tile(np.geomspace(0.001, 3.0, M).reshape(1, 1, 1, 1, M), (1, 1, K, H, 1)), dtype=jnp.float32)
        decay_slopes = jnp.asarray(np.log(np.expm1(np.geomspace(0.001, 0.1, N_DECAY))), dtype=jnp.float32)
        anchor_slopes = jnp.asarray(np.log(np.expm1(np.geomspace(0.01, 0.1, 4))), dtype=jnp.float32)
        score_scale = jnp.ones((K,), dtype=jnp.float32)
        g = np.sqrt(2.0 / (H + DIM_SWIGLU))
        W_re = jax.random.normal(ks[4], (K, H, DIM_SWIGLU), dtype=jnp.float32) * g
        W_im = jax.random.normal(ks[5], (K, H, DIM_SWIGLU), dtype=jnp.float32) * g
        norm_scale = jnp.ones((1, 1, K, H), dtype=jnp.float32)
        W_out = jax.random.normal(ks[6], (K * H * 3, D), dtype=jnp.float32) / np.sqrt(K * H * 3)
        return {'x': x, 'W_mem': W_mem, 'conv_k': conv_k, 'W_q': W_q, 'theta': theta, 'decay_slopes': decay_slopes, 'anchor_slopes': anchor_slopes, 'score_scale': score_scale, 'W_re': W_re, 'W_im': W_im, 'norm_scale': norm_scale, 'W_out': W_out}
    _L1_attn_all = _L1_attn_setup()
    _L1_attn_in = {k: v for k, v in _L1_attn_all.items() if k in ('W_mem', 'conv_k', 'W_q', 'theta', 'decay_slopes', 'anchor_slopes', 'score_scale', 'W_re', 'W_im', 'norm_scale', 'W_out')}
    del _L1_attn_all

    def _L1_xattn_setup():
        import jax, jax.numpy as jnp
        import numpy as np
        N_HEADS = 16
        N_KV_HEADS = 4
        ROPE_THETA = 10000.0
        EPS = 1e-05

        def _rms_norm(x, w):
            var = jnp.mean(x * x, axis=-1, keepdims=True)
            return x * jax.lax.rsqrt(var + EPS) * w

        def _rope_sin_cos(T, head_dim, dtype):
            inv_freq = 1.0 / ROPE_THETA ** (jnp.arange(0, head_dim, 2, dtype=jnp.float32) / head_dim)
            t = jnp.arange(T, dtype=jnp.float32)
            freqs = jnp.outer(t, inv_freq)
            emb = jnp.concatenate([freqs, freqs], -1)
            return (jnp.sin(emb).astype(dtype)[None, None], jnp.cos(emb).astype(dtype)[None, None])

        def _rotate_half(x):
            h = x.shape[-1] // 2
            x1, x2 = (x[..., :h], x[..., h:])
            return jnp.concatenate([-x2, x1], axis=-1)
        key = jax.random.key(seed)
        ks = jax.random.split(key, 6)
        B, T, C = (2, 256, 256)
        Ckv = C // N_HEADS * N_KV_HEADS
        return {'q': jax.random.normal(ks[0], (B, T, C), jnp.float32), 'k': jax.random.normal(ks[1], (B, T, Ckv), jnp.float32), 'v': jax.random.normal(ks[2], (B, T, Ckv), jnp.float32), 'q_norm_w': jnp.ones((C,), jnp.float32), 'k_norm_w': jnp.ones((Ckv,), jnp.float32), 'w_out': jax.random.normal(ks[3], (C, C), jnp.float32) * C ** (-0.5)}
    _L1_xattn_all = _L1_xattn_setup()
    _L1_xattn_in = {k: v for k, v in _L1_xattn_all.items() if k in ('q_norm_w', 'k_norm_w', 'w_out')}
    del _L1_xattn_all

    def _L1_ffn_setup():
        import jax, jax.numpy as jnp
        import numpy as np
        BLOCK_SIZE = 32
        HIDDEN_SIZE = 256
        MLP_DIM = 2048
        NVFP4_LUT = jnp.array([0.0, 0.5, 1.0, 1.5, 2.0, 3.0, 4.0, 6.0, 0.0, -0.5, -1.0, -1.5, -2.0, -3.0, -4.0, -6.0], dtype=jnp.float32)

        def dequant_nvfp4(W_packed, scales, block=BLOCK_SIZE):
            N = W_packed.shape[0]
            low = W_packed & 15
            high = W_packed >> 4 & 15
            idx = jnp.stack([low, high], axis=-1).reshape(N, -1)
            vals = NVFP4_LUT[idx]
            K = vals.shape[1]
            vals = vals.reshape(N, K // block, block) * scales[:, :, None]
            return vals.reshape(N, K)
        key = jax.random.key(seed)
        ks = jax.random.split(key, 7)
        x = jax.random.normal(ks[0], (4, 32, HIDDEN_SIZE), dtype=jnp.float32)
        gate_W_packed = jax.random.randint(ks[1], (MLP_DIM, HIDDEN_SIZE // 2), 0, 32, dtype=jnp.int32)
        gate_scales = jax.random.uniform(ks[2], (MLP_DIM, HIDDEN_SIZE // BLOCK_SIZE), dtype=jnp.float32) * 0.1 + 0.001
        up_W_packed = jax.random.randint(ks[3], (MLP_DIM, HIDDEN_SIZE // 2), 0, 32, dtype=jnp.int32)
        up_scales = jax.random.uniform(ks[4], (MLP_DIM, HIDDEN_SIZE // BLOCK_SIZE), dtype=jnp.float32) * 0.1 + 0.001
        down_W_packed = jax.random.randint(ks[5], (HIDDEN_SIZE, MLP_DIM // 2), 0, 32, dtype=jnp.int32)
        down_scales = jax.random.uniform(ks[6], (HIDDEN_SIZE, MLP_DIM // BLOCK_SIZE), dtype=jnp.float32) * 0.1 + 0.001
        return {'x': x, 'gate_W_packed': gate_W_packed, 'gate_scales': gate_scales, 'up_W_packed': up_W_packed, 'up_scales': up_scales, 'down_W_packed': down_W_packed, 'down_scales': down_scales}
    _L1_ffn_all = _L1_ffn_setup()
    _L1_ffn_in = {k: v for k, v in _L1_ffn_all.items() if k in ('gate_W_packed', 'gate_scales', 'up_W_packed', 'up_scales', 'down_W_packed', 'down_scales')}
    del _L1_ffn_all
    return {'x': x, 'ctx_512': ctx_512, 'L0_attn_W_Q': _L0_attn_in['W_Q'], 'L0_attn_W_K': _L0_attn_in['W_K'], 'L0_attn_W_V': _L0_attn_in['W_V'], 'L0_attn_W_O': _L0_attn_in['W_O'], 'L0_attn_b_Q': _L0_attn_in['b_Q'], 'L0_attn_b_K': _L0_attn_in['b_K'], 'L0_attn_b_V': _L0_attn_in['b_V'], 'L0_attn_b_O': _L0_attn_in['b_O'], 'L0_ffn_ln1_w': _L0_ffn_in['ln1_w'], 'L0_ffn_ln2_w': _L0_ffn_in['ln2_w'], 'L0_ffn_Wq': _L0_ffn_in['Wq'], 'L0_ffn_Wk': _L0_ffn_in['Wk'], 'L0_ffn_Wv': _L0_ffn_in['Wv'], 'L0_ffn_Wo': _L0_ffn_in['Wo'], 'L0_ffn_A': _L0_ffn_in['A'], 'L0_ffn_B': _L0_ffn_in['B'], 'L0_ffn_W_in_base': _L0_ffn_in['W_in_base'], 'L0_ffn_W_up_base': _L0_ffn_in['W_up_base'], 'L0_ffn_W_down': _L0_ffn_in['W_down'], 'L1_attn_W_mem': _L1_attn_in['W_mem'], 'L1_attn_conv_k': _L1_attn_in['conv_k'], 'L1_attn_W_q': _L1_attn_in['W_q'], 'L1_attn_theta': _L1_attn_in['theta'], 'L1_attn_decay_slopes': _L1_attn_in['decay_slopes'], 'L1_attn_anchor_slopes': _L1_attn_in['anchor_slopes'], 'L1_attn_score_scale': _L1_attn_in['score_scale'], 'L1_attn_W_re': _L1_attn_in['W_re'], 'L1_attn_W_im': _L1_attn_in['W_im'], 'L1_attn_norm_scale': _L1_attn_in['norm_scale'], 'L1_attn_W_out': _L1_attn_in['W_out'], 'L1_xattn_q_norm_w': _L1_xattn_in['q_norm_w'], 'L1_xattn_k_norm_w': _L1_xattn_in['k_norm_w'], 'L1_xattn_w_out': _L1_xattn_in['w_out'], 'L1_ffn_gate_W_packed': _L1_ffn_in['gate_W_packed'], 'L1_ffn_gate_scales': _L1_ffn_in['gate_scales'], 'L1_ffn_up_W_packed': _L1_ffn_in['up_W_packed'], 'L1_ffn_up_scales': _L1_ffn_in['up_scales'], 'L1_ffn_down_W_packed': _L1_ffn_in['down_W_packed'], 'L1_ffn_down_scales': _L1_ffn_in['down_scales']}

def reference(x, ctx_512, L0_attn_W_Q, L0_attn_W_K, L0_attn_W_V, L0_attn_W_O, L0_attn_b_Q, L0_attn_b_K, L0_attn_b_V, L0_attn_b_O, L0_ffn_ln1_w, L0_ffn_ln2_w, L0_ffn_Wq, L0_ffn_Wk, L0_ffn_Wv, L0_ffn_Wo, L0_ffn_A, L0_ffn_B, L0_ffn_W_in_base, L0_ffn_W_up_base, L0_ffn_W_down, L1_attn_W_mem, L1_attn_conv_k, L1_attn_W_q, L1_attn_theta, L1_attn_decay_slopes, L1_attn_anchor_slopes, L1_attn_score_scale, L1_attn_W_re, L1_attn_W_im, L1_attn_norm_scale, L1_attn_W_out, L1_xattn_q_norm_w, L1_xattn_k_norm_w, L1_xattn_w_out, L1_ffn_gate_W_packed, L1_ffn_gate_scales, L1_ffn_up_W_packed, L1_ffn_up_scales, L1_ffn_down_W_packed, L1_ffn_down_scales):
    import jax
    import jax.numpy as jnp

    def _L0_attn_ref(x, W_Q, W_K, W_V, W_O, b_Q, b_K, b_V, b_O):
        import jax, jax.numpy as jnp
        import numpy as np
        BATCH, SEQ, D_MODEL, N_HEADS, D_HEAD = (2, 256, 256, 16, 128)
        ATTN_SCALE = np.sqrt(D_HEAD).astype(np.float32)
        IGNORE = jnp.float32(-100000.0)
        q = jnp.einsum('bpd,hde->bphe', x, W_Q) + b_Q
        k = jnp.einsum('bpd,hde->bphe', x, W_K) + b_K
        v = jnp.einsum('bpd,hde->bphe', x, W_V) + b_V
        scores = jnp.einsum('bqhe,bkhe->bhqk', q, k) / ATTN_SCALE
        S = x.shape[1]
        causal = jnp.tril(jnp.ones((S, S), bool))
        scores = jnp.where(causal, scores, IGNORE)
        attn = jax.nn.softmax(scores, axis=-1)
        z = jnp.einsum('bkhe,bhqk->bqhe', v, attn)
        out = jnp.einsum('bqhe,hed->bqd', z, W_O) + b_O
        return out

    def _L0_xattn_ref(q, k, v):
        import jax, jax.numpy as jnp
        import numpy as np
        import math
        NUM_Q_HEADS = 32
        NUM_KV_HEADS = 8
        B, S, E = q.shape
        H, KV = (NUM_Q_HEADS, NUM_KV_HEADS)
        D = E // H
        G = H // KV
        scale = math.sqrt(D)
        qh = q.reshape(B, S, KV, G, D).transpose(0, 2, 3, 1, 4)
        kh = k.reshape(B, S, KV, D).transpose(0, 2, 1, 3)
        vh = v.reshape(B, S, KV, D).transpose(0, 2, 1, 3)
        scores = jnp.einsum('bkgsd,bktd->bkgst', qh, kh) / scale
        weights = jax.nn.softmax(scores, axis=-1)
        out = jnp.einsum('bkgst,bktd->bkgsd', weights, vh)
        return out.transpose(0, 3, 1, 2, 4).reshape(B, S, E)

    def _L0_ffn_ref(hidden_states, ln1_w, ln2_w, Wq, Wk, Wv, Wo, A, B, W_in_base, W_up_base, W_down):
        import jax, jax.numpy as jnp
        import numpy as np
        B_, S, D = (2, 256, 256)
        F_ = 1024
        R = 16
        H = 16
        HD = D // H
        MOD_SCALE = 0.1
        EPS = 1e-06

        def _rmsnorm(x, w):
            v = jnp.mean(x * x, axis=-1, keepdims=True)
            return x * jax.lax.rsqrt(v + EPS) * w

        def _attention(x, Wq, Wk, Wv, Wo):
            b, s, d = x.shape
            q = (x @ Wq.T).reshape(b, s, H, HD)
            k = (x @ Wk.T).reshape(b, s, H, HD)
            v = (x @ Wv.T).reshape(b, s, H, HD)
            scores = jnp.einsum('bqhd,bkhd->bhqk', q, k) / np.sqrt(HD).astype(np.float32)
            causal = jnp.tril(jnp.ones((s, s), bool))
            scores = jnp.where(causal, scores, jnp.finfo(scores.dtype).min)
            probs = jax.nn.softmax(scores, axis=-1)
            out = jnp.einsum('bhqk,bkhd->bqhd', probs, v).reshape(b, s, d)
            return out @ Wo.T
        residual = hidden_states
        x = _rmsnorm(hidden_states, ln1_w)
        attn = _attention(x, Wq, Wk, Wv, Wo)
        mod = MOD_SCALE * jnp.tanh(attn @ A)
        h = _rmsnorm(residual, ln2_w)
        gate_pre = h @ W_in_base.T + mod * (h @ A) @ B
        gate = jax.nn.silu(gate_pre)
        up = h @ W_up_base.T
        mlp_out = gate * up @ W_down.T
        return residual + mlp_out

    def _L1_attn_ref(x, W_mem, conv_k, W_q, theta, decay_slopes, anchor_slopes, score_scale, W_re, W_im, norm_scale, W_out):
        import jax, jax.numpy as jnp
        import numpy as np
        from jax import lax
        B, L, D = (2, 512, 256)
        K, KQ, M, H = (32, 4, 8, 8)
        MEM = K * H
        FLAT = K * H * M
        CONV_W = 4
        DIM_SWIGLU = H * 3 * 2
        N_DECAY = K - 4

        def _forward(x, W_mem, conv_k, W_q, theta, decay_slopes, anchor_slopes, score_scale, W_re, W_im, norm_scale, W_out):
            b, l, d = x.shape
            z = x @ W_mem
            z = lax.conv_general_dilated(z, conv_k, window_strides=(1,), padding=[(CONV_W - 1, 0)], dimension_numbers=('NHC', 'HIO', 'NHC'), feature_group_count=MEM + K)
            k_val = z[..., :MEM].reshape(b, l, K, H)
            s_raw = z[..., MEM:].reshape(b, l, K, 1)
            q = (x @ W_q).reshape(b, l, KQ, H, M, 2)
            q_re, q_im = (q[..., 0], q[..., 1])
            pos = jnp.arange(l, dtype=jnp.float32)
            slopes_d = jax.nn.softplus(decay_slopes).reshape(1, 1, -1, 1)
            slopes_a = jax.nn.softplus(anchor_slopes).reshape(1, 1, -1, 1)
            dist = jnp.maximum(jnp.float32(l - 1) - pos, 0.0)
            log_w = jnp.concatenate([-slopes_d * dist[None, :, None, None], -slopes_a * pos[None, :, None, None]], axis=2)
            log_p = jnp.clip(score_scale[None, None, :, None] * s_raw, -20.0, 20.0)
            p_w = jnp.exp(log_p + log_w)
            phi = k_val[..., None] * theta
            re_k, im_k = (jnp.cos(phi), jnp.sin(phi))
            pw5 = p_w[..., None]
            merged = jnp.concatenate([p_w.squeeze(-1), (pw5 * re_k).reshape(b, l, FLAT), (pw5 * im_k).reshape(b, l, FLAT)], axis=-1)
            cs = jnp.cumsum(merged, axis=1)
            den = cs[..., :K]
            num_re = cs[..., K:K + FLAT]
            num_im = cs[..., K + FLAT:]
            inv_den = 1.0 / jnp.maximum(den[..., None], 0.0001)
            state_re = num_re.reshape(b, l, K, H, M) * inv_den[..., None]
            state_im = num_im.reshape(b, l, K, H, M) * inv_den[..., None]
            n_rep = K // KQ
            q_re = jnp.repeat(q_re, n_rep, axis=2)
            q_im = jnp.repeat(q_im, n_rep, axis=2)
            out_re = jnp.sum(state_re * q_re + state_im * q_im, axis=-1)
            out_im = jnp.sum(state_im * q_re - state_re * q_im, axis=-1)
            out_re = out_re * norm_scale
            out_im = out_im * norm_scale
            y = jnp.einsum('blkh,khn->blkn', out_re, W_re) + jnp.einsum('blkh,khn->blkn', out_im, W_im)
            y_val, y_gate = jnp.split(y, 2, axis=-1)
            y = (y_val * jax.nn.silu(y_gate)).reshape(b, l, -1)
            return y @ W_out
        return _forward(x, W_mem, conv_k, W_q, theta, decay_slopes, anchor_slopes, score_scale, W_re, W_im, norm_scale, W_out)

    def _L1_xattn_ref(q, k, v, q_norm_w, k_norm_w, w_out):
        import jax, jax.numpy as jnp
        import numpy as np
        N_HEADS = 16
        N_KV_HEADS = 4
        ROPE_THETA = 10000.0
        EPS = 1e-05

        def _rms_norm(x, w):
            var = jnp.mean(x * x, axis=-1, keepdims=True)
            return x * jax.lax.rsqrt(var + EPS) * w

        def _rope_sin_cos(T, head_dim, dtype):
            inv_freq = 1.0 / ROPE_THETA ** (jnp.arange(0, head_dim, 2, dtype=jnp.float32) / head_dim)
            t = jnp.arange(T, dtype=jnp.float32)
            freqs = jnp.outer(t, inv_freq)
            emb = jnp.concatenate([freqs, freqs], -1)
            return (jnp.sin(emb).astype(dtype)[None, None], jnp.cos(emb).astype(dtype)[None, None])

        def _rotate_half(x):
            h = x.shape[-1] // 2
            x1, x2 = (x[..., :h], x[..., h:])
            return jnp.concatenate([-x2, x1], axis=-1)
        B, T, C = q.shape
        hd = C // N_HEADS
        g = N_HEADS // N_KV_HEADS
        q = _rms_norm(q, q_norm_w)
        k = _rms_norm(k, k_norm_w)
        q = q.reshape(B, T, N_HEADS, hd).transpose(0, 2, 1, 3)
        k = k.reshape(B, T, N_KV_HEADS, hd).transpose(0, 2, 1, 3)
        v = v.reshape(B, T, N_KV_HEADS, hd).transpose(0, 2, 1, 3)
        sin, cos = _rope_sin_cos(T, hd, q.dtype)
        q = q * cos + _rotate_half(q) * sin
        k = k * cos + _rotate_half(k) * sin
        qg = q.reshape(B, N_KV_HEADS, g, T, hd)
        scale = 1.0 / jnp.sqrt(jnp.asarray(hd, q.dtype))
        scores = jnp.einsum('bgnqd,bgkd->bgnqk', qg, k) * scale
        causal = jnp.tril(jnp.ones((T, T), bool))
        scores = jnp.where(causal, scores, jnp.asarray(-1e+30, scores.dtype))
        attn = jax.nn.softmax(scores, axis=-1)
        out = jnp.einsum('bgnqk,bgkd->bgnqd', attn, v)
        out = out.reshape(B, N_HEADS, T, hd).transpose(0, 2, 1, 3).reshape(B, T, C)
        return out @ w_out.T

    def _L1_ffn_ref(x, gate_W_packed, gate_scales, up_W_packed, up_scales, down_W_packed, down_scales):
        import jax, jax.numpy as jnp
        import numpy as np
        BLOCK_SIZE = 32
        HIDDEN_SIZE = 256
        MLP_DIM = 2048
        NVFP4_LUT = jnp.array([0.0, 0.5, 1.0, 1.5, 2.0, 3.0, 4.0, 6.0, 0.0, -0.5, -1.0, -1.5, -2.0, -3.0, -4.0, -6.0], dtype=jnp.float32)

        def dequant_nvfp4(W_packed, scales, block=BLOCK_SIZE):
            N = W_packed.shape[0]
            low = W_packed & 15
            high = W_packed >> 4 & 15
            idx = jnp.stack([low, high], axis=-1).reshape(N, -1)
            vals = NVFP4_LUT[idx]
            K = vals.shape[1]
            vals = vals.reshape(N, K // block, block) * scales[:, :, None]
            return vals.reshape(N, K)
        B, S, H = x.shape
        xt = x.reshape(B * S, H)
        Wg = dequant_nvfp4(gate_W_packed, gate_scales)
        Wu = dequant_nvfp4(up_W_packed, up_scales)
        Wd = dequant_nvfp4(down_W_packed, down_scales)
        gate = jnp.einsum('th,nh->tn', xt, Wg)
        up = jnp.einsum('th,nh->tn', xt, Wu)
        gelu = jnp.tanh(0.7978845608028654 * (gate + 0.044715 * gate ** 3)) * gate * 0.5 + gate * 0.5
        inter = gelu * up
        out = jnp.einsum('tn,hn->th', inter, Wd)
        return out.reshape(B, S, H)
    x = x + _L0_attn_ref(_layernorm(x, axis=-1), L0_attn_W_Q, L0_attn_W_K, L0_attn_W_V, L0_attn_W_O, L0_attn_b_Q, L0_attn_b_K, L0_attn_b_V, L0_attn_b_O)
    x = x + _L0_xattn_ref(_layernorm(x, axis=-1), ctx_512, ctx_512)
    x = x + _L0_ffn_ref(_layernorm(x, axis=-1), L0_ffn_ln1_w, L0_ffn_ln2_w, L0_ffn_Wq, L0_ffn_Wk, L0_ffn_Wv, L0_ffn_Wo, L0_ffn_A, L0_ffn_B, L0_ffn_W_in_base, L0_ffn_W_up_base, L0_ffn_W_down)
    x = x + _L1_attn_ref(_layernorm(x, axis=-1), L1_attn_W_mem, L1_attn_conv_k, L1_attn_W_q, L1_attn_theta, L1_attn_decay_slopes, L1_attn_anchor_slopes, L1_attn_score_scale, L1_attn_W_re, L1_attn_W_im, L1_attn_norm_scale, L1_attn_W_out)
    x = x + _L1_xattn_ref(_layernorm(x, axis=-1), ctx_512, ctx_512, L1_xattn_q_norm_w, L1_xattn_k_norm_w, L1_xattn_w_out)
    x = x + _L1_ffn_ref(_layernorm(x, axis=-1), L1_ffn_gate_W_packed, L1_ffn_gate_scales, L1_ffn_up_W_packed, L1_ffn_up_scales, L1_ffn_down_W_packed, L1_ffn_down_scales)
    return x

_drawn_inputs = setup_inputs


def setup_inputs(seed=0):
    import zlib

    import numpy as np

    out = dict(_drawn_inputs(seed))
    spreads = {'L0_attn_b_Q': (0.0, 0.1),
     'L0_attn_b_K': (0.0, 2.0),
     'L0_attn_b_V': (0.0, 0.1),
     'L0_attn_b_O': (0.0, 0.1),
     'L0_ffn_ln1_w': (1.0, 0.6),
     'L0_ffn_ln2_w': (1.0, 0.6),
     'L1_attn_score_scale': (1.0, 0.6),
     'L1_attn_norm_scale': (1.0, 0.2),
     'L1_xattn_q_norm_w': (1.0, 0.6),
     'L1_xattn_k_norm_w': (1.0, 0.6)}
    factors = {'L0_ffn_Wq': 200.0,
     'L0_ffn_Wk': 200.0,
     'L0_ffn_Wv': 200.0,
     'L0_ffn_Wo': 200.0,
     'L0_ffn_A': 200.0,
     'L0_ffn_B': 200.0,
     'L1_attn_anchor_slopes': 24.952}
    for name, (base, spread) in spreads.items():
        noise = np.random.default_rng([zlib.crc32(name.encode()), seed]).standard_normal(out[name].shape)
        drawn = base * np.exp(spread * noise) if base else spread * noise
        out[name] = jnp.asarray(drawn.astype(out[name].dtype))
    for name, factor in factors.items():
        out[name] = (out[name] * factor).astype(out[name].dtype)
    return out
```

```python
from contextlib import ExitStack

import numpy as np

import concourse.bass as bass
from concourse import mybir

STAGES = "123456"

ALU = mybir.AluOpType
ACT = mybir.ActivationFunctionType
F32 = mybir.dt.float32
I32 = mybir.dt.int32
AX_X = mybir.AxisListType.X

P = 128
B, S, D = 32, 64, 256
TOK = B * S
NT = TOK // P
NC = D // P
EPS_LN = 1e-5
BIG = 3.0e38


def constant_columns():
    sizes = [("ident", P), ("tri", P), ("mask_L0", S), ("mask_ffn", S), ("mask_L1", S),
             ("blk8", 4), ("blk16", 2), ("rope_cos", 16), ("rope_sin", 16),
             ("age", 512), ("blk_k", 16), ("eps_ln", 1), ("eps_rms", 1), ("eps_rms5", 1), ("half_pi", 1)]
    at, out = 0, {}
    for name, n in sizes:
        out[name] = (at, n)
        at += n
    return out, at


def constants():
    cols, width = constant_columns()
    c = np.zeros((P, width), np.float32)

    def put(name, a):
        at, n = cols[name]
        c[:, at:at + n] = np.asarray(a, np.float32).reshape(P, n) if np.ndim(a) else a

    p = np.arange(P)
    put("ident", np.eye(P))
    put("tri", (p[:, None] <= p[None, :]) & (p[:, None] // S == p[None, :] // S))
    seen = np.arange(S)[None, :] <= (p % S)[:, None]
    put("mask_L0", np.where(seen, BIG, -1e5 * np.sqrt(128.0)))
    put("mask_ffn", np.where(seen, BIG, -BIG))
    put("mask_L1", np.where(seen, BIG, -4e30))
    put("blk8", (p[:, None] % 32) // 8 == np.arange(4)[None, :])
    put("blk16", (p[:, None] % 32) // 16 == np.arange(2)[None, :])
    inv = np.float32(1.0) / np.float32(10000.0) ** (np.arange(0, 16, 2, dtype=np.float32) / np.float32(16))
    ang = (p % S).astype(np.float32)[:, None] * inv[None, :]
    put("rope_cos", np.concatenate([np.cos(ang), np.cos(ang)], 1))
    put("rope_sin", np.concatenate([-np.sin(ang), np.sin(ang)], 1))
    l = np.arange(512) % S
    put("age", np.where(p[:, None] < 28, -(S - 1 - l)[None, :], -l[None, :]))
    put("blk_k", p[:, None] // 8 == np.arange(16)[None, :])
    put("eps_ln", EPS_LN)
    put("eps_rms", 1e-6)
    put("eps_rms5", 1e-5)
    put("half_pi", np.pi / 2)
    return c


def run_steps(eng, n, parts, unroll=2, head=None):
    last = max(lag for _, lag in parts)
    if head is None:
        head = unroll * (1 + -(-(last + 2) // unroll))
    turns = (n - head) // unroll
    if turns < 2:
        head, turns = n + last, 0

    def step(s):
        for part, lag in parts:
            if 0 <= s - lag < n:
                part(s - lag, (s - lag) // unroll, (s - lag) % unroll)

    for s in range(min(head, n + last)):
        step(s)
    if not turns:
        return
    with eng.Fori(0, turns) as r:
        for j in range(unroll):
            for part, lag in parts:
                at = head + j - lag
                part(r * unroll + at, r + at // unroll, at % unroll)
    for s in range(head + turns * unroll, n + last):
        step(s)


def wait(eng, sem, value):
    if isinstance(value, int) and value <= 0:
        return
    eng.wait_ge(sem, value)


def bc(ap, shape):
    return ap.to_broadcast(shape)


class Core:

    def __init__(self, nc, ctx, ins):
        self.nc, self.ins, self.ctx = nc, ins, ctx
        self.cols, width = constant_columns()
        self.x = ctx.enter_context(nc.sbuf_tensor("x_rows", [P, NT, D], F32))
        self.const = ctx.enter_context(nc.sbuf_tensor("const", [P, width], F32))

    def c(self, name, rows=P):
        at, n = self.cols[name]
        return self.const[0:rows, at:at + n]


class Room:

    used = []
    kept = None

    def __init__(self, nc, ctx, tag):
        self.nc, self.ctx, self.tag = nc, ctx, tag

    def sb(self, name, shape, dt=F32):
        return self.ctx.enter_context(self.nc.sbuf_tensor(f"{self.tag}_{name}", shape, dt))

    def ps(self, name, shape):
        return self.ctx.enter_context(self.nc.psum_tensor(f"{self.tag}_{name}", shape, F32))

    def sems(self, *names):
        made = [Room.kept.enter_context(self.nc.semaphore(f"{self.tag}_{n}")) for n in names]
        Room.used += made
        return made


def run_stage(core, stage):
    nc = core.nc
    with ExitStack() as ctx:
        Room.kept, Room.used = ctx, []
        stage(core)
        block = ctx.enter_context(nc.Block())
        numbers = sorted(s.num for s in Room.used)

        @block.sync
        def _(sp):
            first = 0
            for n in range(1, len(numbers) + 1):
                if n == len(numbers) or numbers[n] != numbers[n - 1] + 1:
                    sp.sem_clear(range(numbers[first], numbers[n - 1] + 1))
                    first = n


def token_stats(core, mv, rstd, tag, rms_eps=None, factor=None):
    nc = core.nc
    with ExitStack() as ctx:
        room = Room(nc, ctx, tag)
        stats = room.sb("stats", [P, NT, 6])
        std = room.sb("std", [P, NT])
        half = room.sb("half", [P, NT])
        square = room.sb("square", [P, NT])
        root = room.sb("root", [P, NT])
        inv = room.sb("inv", [P, NT])
        stats_done, mv_done, std_done, rstd_done, square_done, root_done, inv_done = room.sems(
            "stats_done", "mv_done", "std_done", "rstd_done", "square_done", "root_done", "inv_done")
        block = ctx.enter_context(nc.Block())

        @block.vector
        def _(dve):
            with dve.Fori(0, NT) as t:
                nc.vector.bn_stats(stats[:, t, :], core.x[:, t, :]).then_inc(stats_done, 1)
            dve.wait_ge(stats_done, NT)
            for t in range(NT):
                nc.vector.bn_aggr(mv[:, t, :], stats[:, t, :]).then_inc(mv_done, 1)
            dve.wait_ge(std_done, 1)
            nc.vector.reciprocal(rstd[:, :], std[:, :]).then_inc(rstd_done, 1)
            if rms_eps is None:
                return
            dve.wait_ge(rstd_done, 1)
            dve.wait_ge(mv_done, NT)
            nc.vector.tensor_tensor(half[:, :], mv[:, :, 1], rstd[:, :], ALU.mult).then_inc(square_done, 1)
            dve.wait_ge(square_done, 1)
            nc.vector.tensor_tensor(square[:, :], half[:, :], rstd[:, :], ALU.mult).then_inc(square_done, 1)
            dve.wait_ge(root_done, 1)
            nc.vector.reciprocal(inv[:, :], root[:, :]).then_inc(inv_done, 1)
            dve.wait_ge(inv_done, 1)
            nc.vector.tensor_tensor(factor[:, :], inv[:, :], rstd[:, :], ALU.mult).then_inc(inv_done, 1)

        @block.scalar
        def _(act):
            act.wait_ge(mv_done, NT)
            nc.scalar.activation(std[:, :], mv[:, :, 1], ACT.Sqrt, bias=core.c("eps_ln")).then_inc(std_done, 1)
            if rms_eps is not None:
                act.wait_ge(square_done, 2)
                nc.scalar.activation(root[:, :], square[:, :], ACT.Sqrt, bias=core.c(rms_eps)).then_inc(root_done, 1)


def turn_tokens(core, xnT, mv, factor, tag, column_step=1):
    nc = core.nc
    with ExitStack() as ctx:
        room = Room(nc, ctx, tag)
        xn = room.sb("xn", [P, 4, D])
        turned = room.ps("turned", [P, 4, 512])
        xn_done, turned_done, out_act, out_dve = room.sems("xn_done", "turned_done", "out_act", "out_dve")
        block = ctx.enter_context(nc.Block())

        @block.vector
        def _(dve):
            def evacuate_odd(t):
                dve.wait_ge(turned_done, t + 1)
                nc.vector.tensor_copy(xnT[:, :, t, :], turned[:, t % 4, 0:D].rearrange("p (c q) -> p c q", c=NC)) \
                    .then_inc(out_dve, 1)

            for t in range(NT):
                if t >= 4:
                    dve.wait_ge(turned_done, t - 3)
                nc.vector.tensor_scalar(xn[:, t % 4, :], core.x[:, t, :], mv[:, t, 0:1], factor[:, t:t + 1],
                                        ALU.subtract, ALU.mult).then_inc(xn_done, 1)
                if t % 2 and t >= 3:
                    evacuate_odd(t - 2)
            evacuate_odd(NT - 1)

        @block.scalar
        def _(act):
            for t in range(0, NT, 2):
                act.wait_ge(turned_done, t + 1)
                nc.scalar.activation(xnT[:, :, t, :], turned[:, t % 4, 0:D].rearrange("p (c q) -> p c q", c=NC),
                                     ACT.Copy).then_inc(out_act, 1)

        @block.tensor
        def _(pe):
            for t in range(NT):
                pe.wait_ge(xn_done, t + 1)
                if t >= 4:
                    pe.wait_ge(out_dve if t % 2 else out_act, (t - 4) // 2 + 1)
                for c in range(NC):
                    cols = slice(c, D, 2) if column_step == 2 else slice(c * P, (c + 1) * P)
                    last = nc.tensor.transpose(turned[:, t % 4, c * P:(c + 1) * P], xn[:, t % 4, cols],
                                               core.c("ident"))
                last.then_inc(turned_done, 1)


def stage_L0_attention(core):
    nc, ins = core.nc, core.ins
    H, E = 16, 128
    G = 4
    TG = NT // G
    U = H * G
    SCALE = float(1.0 / np.sqrt(np.float32(E)))
    with ExitStack() as octx:
        oroom = Room(nc, octx, "s1")
        xnT = oroom.sb("xnT", [P, NC, NT, P])
        mv = oroom.sb("mv", [P, NT, 2])
        rstd = oroom.sb("rstd", [P, NT])
        token_stats(core, mv, rstd, "s1n")
        turn_tokens(core, xnT, mv, rstd, "s1t")
        with ExitStack() as ctx:
            room = Room(nc, ctx, "s1")
            wq = room.sb("wq", [P, 2, NC, E])
            wk = room.sb("wk", [P, 2, NC, E])
            wv = room.sb("wv", [P, 2, NC, E])
            wo = room.sb("wo", [P, 2, D])
            bias = room.sb("bias", [P, 2, 3])
            bo = room.sb("bo", [P, D])
            qT = room.sb("qT", [P, TG * P])
            kT = room.sb("kT", [P, TG * P])
            v = room.sb("v", [P, 2, TG * E])
            sc = room.sb("sc", [P, TG, S])
            ex = room.sb("ex", [P, TG, S])
            mx = room.sb("mx", [P, TG])
            sm = room.sb("sm", [P, TG])
            rs = room.sb("rs", [P, TG])
            prob = room.sb("prob", [P, TG, P])
            probT = room.sb("probT", [P, TG * P])
            zT = room.sb("zT", [P, TG * P])
            q_ps = room.ps("q_ps", [P, 512])
            k_ps = room.ps("k_ps", [P, 512])
            v_ps = room.ps("v_ps", [P, 512])
            s_ps = room.ps("s_ps", [P, 512])
            pT_ps = room.ps("pT_ps", [P, 512])
            z_ps = room.ps("z_ps", [P, 512])
            o_ps = room.ps("o_ps", [P, 2, 512])
            (w_in0, w_in1, bias_in0, bias_in1, bo_in, q_full, k_full, v_full, s_full, pT_full, z_full, o_full, q_out, k_out, v_out,
             masked, maxed, shifted, exped, summed, inverted, prob_done, pT_out, z_out, o_out, zeroed) = room.sems(
                "w_in0", "w_in1", "bias_in0", "bias_in1", "bo_in", "q_full", "k_full", "v_full", "s_full", "pT_full", "z_full", "o_full",
                "q_out", "k_out", "v_out", "masked", "maxed", "shifted", "exped", "summed", "inverted",
                "prob_done", "pT_out", "z_out", "o_out", "zeroed")
            w_in, bias_in = (w_in0, w_in1), (bias_in0, bias_in1)
            block = ctx.enter_context(nc.Block())

            @block.sync
            def _(sp):
                sp.dma_start(bo[:, :], ins["L0_attn_b_O"].rearrange("(a n) -> a n", a=1).to_broadcast([P, D])) \
                    .then_inc(bo_in, 16)

                def load(h, rnd, slot):
                    wait(sp, o_full, (h - 2) * G + G)
                    src = ins["bias_L0"].rearrange("h e b -> e h b")
                    sp.dma_start(bias[:, slot:slot + 1, :], src[:, bass.ds(h, 1), :]).then_inc(bias_in[slot], 16)
                    for dst, name in ((wq, "L0_attn_W_Q"), (wk, "L0_attn_W_K"), (wv, "L0_attn_W_V")):
                        src = ins[name].rearrange("h (c p) e -> p (h c) e", p=P)
                        sp.dma_start(dst[:, slot, :, :], src[:, bass.ds(h * NC, NC), :]).then_inc(w_in[slot], 16)
                    src = ins["L0_attn_W_O"].rearrange("h e n -> e h n")
                    sp.dma_start(wo[:, slot:slot + 1, :], src[:, bass.ds(h, 1), :]).then_inc(w_in[slot], 16)

                run_steps(sp, H, [(load, 0)], unroll=2)

            @block.tensor
            def _(pe):
                def project(u, rnd, k):
                    g, slot = k % G, k // G
                    if g == 0:
                        pe.wait_ge(w_in[slot], (rnd + 1) * 64)
                    for w, ps, full, out in ((wq, q_ps, q_full, q_out), (wk, k_ps, k_full, k_out)):
                        wait(pe, out, u)
                        for c in range(NC):
                            last = nc.tensor.matmul(ps[:, :], w[:, slot, c, :], xnT[:, c, g * TG:(g + 1) * TG, :],
                                                    start=(c == 0), stop=(c == NC - 1))
                        last.then_inc(full, 1)
                    wait(pe, v_out, u)
                    for t in range(TG):
                        for c in range(NC):
                            last = nc.tensor.matmul(v_ps[:, t * E:(t + 1) * E], xnT[:, c, g * TG + t, :],
                                                    wv[:, slot, c, :], start=(c == 0), stop=(c == NC - 1))
                    last.then_inc(v_full, 1)

                def scores(u, rnd, k):
                    pe.wait_ge(q_out, u + 1)
                    pe.wait_ge(k_out, u + 1)
                    wait(pe, masked, u)
                    for t in range(TG):
                        for b in range(2):
                            at = t * P + b * S
                            last = nc.tensor.matmul(s_ps[b * S:(b + 1) * S, t * S:(t + 1) * S], qT[:, at:at + S],
                                                    kT[:, at:at + S], start=True, stop=True)
                    last.then_inc(s_full, 1)

                def turn(u, rnd, k):
                    pe.wait_ge(prob_done, u + 1)
                    wait(pe, pT_out, u)
                    for t in range(TG):
                        last = nc.tensor.transpose(pT_ps[:, t * P:(t + 1) * P], prob[:, t, :], core.c("ident"))
                    last.then_inc(pT_full, 1)

                def weigh(u, rnd, k):
                    pe.wait_ge(pT_out, u + 1)
                    pe.wait_ge(v_out, u + 1)
                    wait(pe, z_out, u)
                    for t in range(TG):
                        last = nc.tensor.matmul(z_ps[:, t * P:(t + 1) * P], v[:, k % 2, t * E:(t + 1) * E],
                                                probT[:, t * P:(t + 1) * P], start=True, stop=True)
                    last.then_inc(z_full, 1)

                def output(u, rnd, k):
                    pe.wait_ge(z_out, u + 1)
                    wait(pe, o_out, u)
                    for t in range(TG):
                        last = nc.tensor.matmul(o_ps[:, t // 2, (t % 2) * D:(t % 2 + 1) * D], zT[:, t * P:(t + 1) * P],
                                                wo[:, k // G, :], start=True, stop=True)
                    last.then_inc(o_full, 1)

                run_steps(pe, U, [(project, 0), (turn, 1), (scores, 0), (output, 2), (weigh, 1)], unroll=8)

            @block.scalar
            def _(act):
                def q_copy(u, rnd, k):
                    act.wait_ge(bias_in[k // G], (rnd + 1) * 16)
                    act.wait_ge(q_full, u + 1)
                    nc.scalar.activation(qT[:, :], q_ps[:, :], ACT.Identity, bias=bias[:, k // G, 0:1]) \
                        .then_inc(q_out, 1)

                def exponent(u, rnd, k):
                    act.wait_ge(shifted, u + 1)
                    nc.scalar.activation(ex[:, :, :], sc[:, :, :], ACT.Exp, scale=SCALE).then_inc(exped, 1)

                def probT_copy(u, rnd, k):
                    act.wait_ge(pT_full, u + 1)
                    nc.scalar.activation(probT[:, :], pT_ps[:, :], ACT.Copy).then_inc(pT_out, 1)

                def z_copy(u, rnd, k):
                    act.wait_ge(z_full, u + 1)
                    nc.scalar.activation(zT[:, :], z_ps[:, :], ACT.Identity, bias=bias[:, k // G, 2:3]) \
                        .then_inc(z_out, 1)

                run_steps(act, U, [(q_copy, 0), (probT_copy, 1), (exponent, 0), (z_copy, 1)], unroll=8)

            @block.vector
            def _(dve):
                nc.vector.memset(prob[:, :, :], 0.0).then_inc(zeroed, 1)
                dve.wait_ge(zeroed, 1)
                dve.wait_ge(bo_in, 16)
                for t in range(NT):
                    last = nc.vector.tensor_tensor(core.x[:, t, :], core.x[:, t, :], bo[:, :], ALU.add)
                last.then_inc(zeroed, 1)
                dve.wait_ge(zeroed, 2)

                def k_copy(u, rnd, k):
                    dve.wait_ge(bias_in[k // G], (rnd + 1) * 16)
                    dve.wait_ge(k_full, u + 1)
                    nc.vector.tensor_scalar(kT[:, :], k_ps[:, :], bias[:, k // G, 1:2], None, ALU.add) \
                        .then_inc(k_out, 1)

                def v_copy(u, rnd, k):
                    dve.wait_ge(v_full, u + 1)
                    nc.vector.tensor_copy(v[:, k % 2, :], v_ps[:, :]).then_inc(v_out, 1)

                def shift(u, rnd, k):
                    dve.wait_ge(s_full, u + 1)
                    nc.vector.tensor_tensor(sc[:, :, :], s_ps[:, 0:TG * S].rearrange("p (t s) -> p t s", t=TG),
                                            core.c("mask_L0").unsqueeze(1).to_broadcast([P, TG, S]), ALU.min) \
                        .then_inc(masked, 1)
                    dve.wait_ge(masked, u + 1)
                    nc.vector.tensor_reduce(mx[:, :], sc[:, :, :], AX_X, ALU.max).then_inc(maxed, 1)
                    dve.wait_ge(maxed, u + 1)
                    nc.vector.tensor_tensor(sc[:, :, :], sc[:, :, :], mx[:, :].unsqueeze(2).to_broadcast([P, TG, S]),
                                            ALU.subtract).then_inc(shifted, 1)

                def add_out(u, rnd, k):
                    dve.wait_ge(o_full, u + 1)
                    t0 = (k % G) * TG
                    nc.vector.tensor_tensor(core.x[:, t0:t0 + TG, :], core.x[:, t0:t0 + TG, :],
                                            o_ps[:, :, :].rearrange("p b (t n) -> p (b t) n", t=2), ALU.add) \
                        .then_inc(o_out, 1)

                def normalise(u, rnd, k):
                    dve.wait_ge(exped, u + 1)
                    nc.vector.tensor_reduce(sm[:, :], ex[:, :, :], AX_X, ALU.add).then_inc(summed, 1)
                    dve.wait_ge(summed, u + 1)
                    nc.vector.reciprocal(rs[:, :], sm[:, :]).then_inc(inverted, 1)
                    dve.wait_ge(inverted, u + 1)
                    for b in range(2):
                        rows = slice(b * S, (b + 1) * S)
                        last = nc.vector.tensor_tensor(prob[rows, :, b * S:(b + 1) * S], ex[rows, :, :],
                                                       rs[rows, :].unsqueeze(2).to_broadcast([S, TG, S]), ALU.mult)
                    last.then_inc(prob_done, 1)

                run_steps(dve, U, [(k_copy, 0), (v_copy, 0), (shift, 0), (add_out, 2), (normalise, 0)], unroll=8)


def stage_L0_cross(core):
    nc, ins = core.nc, core.ins
    E, KV, GQ = 8, 8, 4
    HEADS = KV * GQ
    SCALE = float(1.0 / np.sqrt(8.0))
    with ExitStack() as octx:
        oroom = Room(nc, octx, "s2")
        mv = oroom.sb("mv", [P, NT, 2])
        rstd = oroom.sb("rstd", [P, NT])
        token_stats(core, mv, rstd, "s2n")
        with ExitStack() as ctx:
            room = Room(nc, ctx, "s2")
            krep = room.sb("krep", [P, 2, 2, P])
            vrow = room.sb("vrow", [P, 2, 2, KV * E])
            kbd = room.sb("kbd", [P, 2, 2, 2, GQ, S])
            vbd = room.sb("vbd", [P, 2, 2, KV, 2, E])
            xn = room.sb("xn", [P, 2, D])
            xT = room.sb("xT", [P, 2, NC, P])
            sc = room.sb("sc", [P, HEADS, S])
            ex = room.sb("ex", [P, 2, HEADS, S])
            mx = room.sb("mx", [P, HEADS])
            sm = room.sb("sm", [P, HEADS])
            rs = room.sb("rs", [P, 2, HEADS])
            probT = room.sb("probT", [P, 2, 8, P])
            att = room.sb("att", [P, D])
            s_ps = room.ps("s_ps", [P, 4, 512])
            pT_ps = room.ps("pT_ps", [P, 2, 512])
            x_ps = room.ps("x_ps", [P, 512])
            o_ps = room.ps("o_ps", [P, 512])
            (k_in0, k_in1, v_in0, v_in1, xn_done, x_full, x_out, kbd_done, vbd_done, s_full, maxed, shifted, exped,
             summed, inverted, pT_full, pT_out, o_full, att_done, att_mid, zeroed) = room.sems(
                "k_in0", "k_in1", "v_in0", "v_in1", "xn_done", "x_full", "x_out", "kbd_done", "vbd_done", "s_full",
                "maxed", "shifted", "exped", "summed", "inverted", "pT_full", "pT_out", "o_full", "att_done",
                "att_mid", "zeroed")
            k_in, v_in = (k_in0, k_in1), (v_in0, v_in1)
            block = ctx.enter_context(nc.Block())

            @block.sync
            def _(sp):
                def load(i, rnd, slot):
                    wait(sp, kbd_done, i - 1)
                    sp.dma_start(krep[:, slot:slot + 1, :, :], ins["ctx_rep8"][bass.ds(i, 1), :, :, :]
                                 .rearrange("t p c k -> p t c k")).then_inc(k_in[slot], 16)
                    wait(sp, vbd_done, i - 1)
                    for half in range(2):
                        sp.dma_start(vrow[half * S:(half + 1) * S, slot, :, :],
                                     ins["ctx_512"].rearrange("b k d -> k b d")[:, bass.ds(i * 2, 2), :]) \
                            .then_inc(v_in[slot], 16)

                run_steps(sp, NT, [(load, 0)])

            @block.vector
            def _(dve):
                nc.vector.memset(vbd[:, :, :, :, :, :], 0.0).then_inc(zeroed, 1)
                dve.wait_ge(zeroed, 1)

                def normalise(i, rnd, k):
                    wait(dve, x_full, i - 1)
                    nc.vector.tensor_scalar(xn[:, k:k + 1, :], core.x[:, bass.ds(i, 1), :], mv[:, bass.ds(i, 1), 0:1],
                                            rstd[:, bass.ds(i, 1)], ALU.subtract, ALU.mult).then_inc(xn_done, 1)

                def spread(i, rnd, k):
                    dve.wait_ge(k_in[k], (rnd + 1) * 16)
                    for c in range(2):
                        for b in range(2):
                            last = nc.vector.tensor_tensor(
                                kbd[:, k, c, b, :, :],
                                krep[:, k, c, b * S:(b + 1) * S].unsqueeze(1).to_broadcast([P, GQ, S]),
                                core.c("blk8").unsqueeze(2).to_broadcast([P, GQ, S]), ALU.mult)
                    last.then_inc(kbd_done, 1)

                def spread_values(i, rnd, k):
                    dve.wait_ge(v_in[k], (rnd + 1) * 32)
                    for half in range(2):
                        rows = slice(half * S, (half + 1) * S)
                        last = nc.vector.tensor_copy(
                            vbd[rows, k, :, :, half, :].rearrange("p b v d -> p (b v) d"),
                            vrow[rows, k, :, :].rearrange("p b (v d) -> p (b v) d", d=E))
                    last.then_inc(vbd_done, 1)

                def shift(i, rnd, k):
                    dve.wait_ge(s_full, i + 1)
                    s = s_ps[:, :, :].rearrange("p j (h s) -> p (j h) s", s=S)
                    nc.vector.tensor_reduce(mx[:, :], s, AX_X, ALU.max).then_inc(maxed, 1)
                    dve.wait_ge(maxed, i + 1)
                    wait(dve, exped, i)
                    nc.vector.tensor_tensor(sc[:, :, :], s, mx[:, :].unsqueeze(2).to_broadcast([P, HEADS, S]),
                                            ALU.subtract).then_inc(shifted, 1)

                def denominators(i, rnd, k):
                    dve.wait_ge(exped, i + 1)
                    nc.vector.tensor_reduce(sm[:, :], ex[:, k, :, :], AX_X, ALU.add).then_inc(summed, 1)
                    dve.wait_ge(summed, i + 1)
                    nc.vector.reciprocal(rs[:, k, :], sm[:, :]).then_inc(inverted, 1)

                def add(i, rnd, k):
                    dve.wait_ge(o_full, i + 1)
                    dve.wait_ge(inverted, i + 1)
                    wait(dve, att_done, i)
                    for c in range(2):
                        o = o_ps[:, c * P:(c + 1) * P].rearrange("p (j g d) -> p j g d", j=4, g=GQ)
                        r = rs[:, k, :].rearrange("p (j c g) -> p c j g", j=4, c=2)[:, c, :, :]
                        last = nc.vector.tensor_tensor(
                            att[:, c * P:(c + 1) * P].rearrange("p (j g d) -> p j g d", j=4, g=GQ), o,
                            r.unsqueeze(3).to_broadcast([P, 4, GQ, E]), ALU.mult)
                    last.then_inc(att_mid, 1)
                    dve.wait_ge(att_mid, i + 1)
                    nc.vector.tensor_tensor(core.x[:, bass.ds(i, 1), :], core.x[:, bass.ds(i, 1), :],
                                            att[:, :].unsqueeze(1), ALU.add).then_inc(att_done, 1)

                run_steps(dve, NT, [(normalise, 0), (spread, 0), (add, 4), (denominators, 2), (spread_values, 2),
                                    (shift, 1)])

            @block.scalar
            def _(act):
                def xT_copy(i, rnd, k):
                    act.wait_ge(x_full, i + 1)
                    wait(act, s_full, i - 1)
                    nc.scalar.activation(xT[:, k, :, :], x_ps[:, 0:D].rearrange("p (c q) -> p c q", c=NC), ACT.Copy) \
                        .then_inc(x_out, 1)

                def exponent(i, rnd, k):
                    act.wait_ge(shifted, i + 1)
                    wait(act, pT_full, 2 * (i - 1))
                    wait(act, inverted, i - 1)
                    nc.scalar.activation(ex[:, k, :, :], sc[:, :, :], ACT.Exp, scale=SCALE).then_inc(exped, 1)

                def probT_copy(half):
                    def part(i, rnd, k):
                        act.wait_ge(pT_full, 2 * i + half + 1)
                        wait(act, o_full, i) if half else None
                        nc.scalar.activation(probT[:, half, :, :], pT_ps[:, :, :].rearrange("p a (b q) -> p (a b) q", q=P),
                                             ACT.Copy).then_inc(pT_out, 1)
                    return part

                run_steps(act, NT, [(xT_copy, 1), (probT_copy(0), 3), (probT_copy(1), 3), (exponent, 1)])

            @block.tensor
            def _(pe):
                def turn_x(i, rnd, k):
                    pe.wait_ge(xn_done, i + 1)
                    wait(pe, x_out, i)
                    for c in range(NC):
                        last = nc.tensor.transpose(x_ps[:, c * P:(c + 1) * P], xn[:, k, c * P:(c + 1) * P],
                                                   core.c("ident"))
                    last.then_inc(x_full, 1)

                def scores(i, rnd, k):
                    pe.wait_ge(x_out, i + 1)
                    pe.wait_ge(kbd_done, i + 1)
                    wait(pe, shifted, i)
                    for b in range(2):
                        for c in range(2):
                            for j in range(4):
                                rows = slice(32 * j, 32 * j + 32)
                                last = nc.tensor.matmul(
                                    s_ps[b * S:(b + 1) * S, j, c * GQ * S:(c + 1) * GQ * S],
                                    xT[rows, k, c, b * S:(b + 1) * S],
                                    kbd[rows, k, c, b, :, :].rearrange("p g s -> p (g s)"), start=True, stop=True)
                    last.then_inc(s_full, 1)

                def turn(half):
                    def part(i, rnd, k):
                        pe.wait_ge(exped, i + 1)
                        wait(pe, pT_out, 2 * i + half)
                        for n in range(8):
                            pair = half * 8 + n
                            last = nc.tensor.transpose(
                                pT_ps[:, n // 4, (n % 4) * P:(n % 4 + 1) * P],
                                ex[:, k, 2 * pair:2 * pair + 2, :].rearrange("p h s -> p (h s)"), core.c("ident"))
                        last.then_inc(pT_full, 1)
                    return part

                def weigh(half):
                    def part(i, rnd, k):
                        pe.wait_ge(pT_out, 2 * i + half + 1)
                        if half == 0:
                            wait(pe, att_mid, i)
                            pe.wait_ge(vbd_done, i + 1)
                        for n in range(8):
                            pair = half * 8 + n
                            j, c, gp = pair // 4, pair // 2 % 2, pair % 2
                            kv = 4 * c + j
                            for b in range(2):
                                at = (kv * GQ + 2 * gp) * E
                                last = nc.tensor.matmul(
                                    o_ps[b * S:(b + 1) * S, at:at + 2 * E], probT[:, half, n, b * S:(b + 1) * S],
                                    vbd[:, k, b, kv, :, :].rearrange("p h d -> p (h d)"), start=True, stop=True)
                        if half:
                            last.then_inc(o_full, 1)
                    return part

                run_steps(pe, NT, [(turn_x, 1), (turn(0), 3), (scores, 1), (turn(1), 3), (weigh(0), 3),
                                   (weigh(1), 3)])


def attention16(core, mode, tag, mv, rstd, factor, w, zT=None, mT=None):
    nc, ins = core.nc, core.ins
    own = mode == "ffn"
    H, E, R = 16, 16, 16
    PAIRS = H // 2
    KV = H if own else 4
    with ExitStack() as ctx:
        room = Room(nc, ctx, tag)
        zt = room.sb("zt", [P, 2, NC, P])
        yt = room.sb("yt", [P, D])
        krow = room.sb("krow", [P, 2, D])
        rot = room.sb("rot", [P, D])
        vrow = room.sb("vrow", [P, 2, 2, KV * E])
        qT = room.sb("qT", [P, 2, NC, P])
        kbd = room.sb("kbd", [P, 2, NC, 2, 2, S])
        vbd = room.sb("vbd", [P, 2, 2, PAIRS if own else KV, 2, E])
        sc = room.sb("sc", [P, H, S])
        ex = room.sb("ex", [P, 2, H, S])
        mx = room.sb("mx", [P, H])
        sm = room.sb("sm", [P, H])
        rs = room.sb("rs", [P, 2, H])
        probT = room.sb("probT", [P, 2, PAIRS // 2, P])
        att = room.sb("att", [P, 2, D])
        attT = room.sb("attT", [P, NC, P])
        th = room.sb("th", [R, P])
        s_ps = room.ps("s_ps", [P, 4, 512])
        pT_ps = room.ps("pT_ps", [P, 512])
        qk_ps = room.ps("qk_ps", [P, 512])
        v_ps = room.ps("v_ps", [P, 512])
        of_ps = room.ps("of_ps", [P, 512])
        o_ps, f_ps = of_ps[:, 0:D], of_ps[:, D:2 * D]

        def upto(n):
            return min(n, NT) if isinstance(n, int) else n

        (ready, y_done, y_added, v_in0, v_in1, qk_full, v_full, q_out, kbd_done, vbd_done, s_full, masked, maxed,
         shifted, exped, summed, inverted, pT_full, pT_out, o_full, att_done, aT_full, aT_out, f_full, tanhed,
         f_out, zeroed) = room.sems(
            "ready", "y_done", "y_added", "v_in0", "v_in1", "qk_full", "v_full", "q_out", "kbd_done", "vbd_done",
            "s_full", "masked", "maxed", "shifted", "exped", "summed", "inverted", "pT_full", "pT_out", "o_full",
            "att_done", "aT_full", "aT_out", "f_full", "tanhed", "f_out", "zeroed")
        v_in = (v_in0, v_in1)
        block = ctx.enter_context(nc.Block())

        if not own:
            @block.sync
            def _(sp):
                def load(i, rnd, slot):
                    wait(sp, vbd_done, i - 1)
                    for half in range(2):
                        sp.dma_start(vrow[half * S:(half + 1) * S, slot, :, :],
                                     ins["ctx_512"].rearrange("b k d -> k b d")[:, bass.ds(i * 2, 2), :]) \
                            .then_inc(v_in[slot], 16)

                run_steps(sp, NT, [(load, 0)])

        @block.vector
        def _(dve):
            nc.vector.memset(vbd[:, :, :, :, :, :], 0.0).then_inc(zeroed, 1)
            dve.wait_ge(zeroed, 1)

            def prepare_own(i, rnd, k):
                wait(dve, v_full, i - 1)
                nc.vector.tensor_scalar(zt[:, k, :, :].unsqueeze(2), zT[:, :, bass.ds(i, 1), :], 1.0, None, ALU.mult) \
                    .then_inc(ready, 1)
                wait(dve, y_added, i)
                nc.vector.tensor_scalar(yt[:, :].unsqueeze(1), core.x[:, bass.ds(i, 1), :], mv[:, bass.ds(i, 1), 0:1],
                                        rstd[:, bass.ds(i, 1)], ALU.subtract, ALU.mult).then_inc(y_done, 1)
                dve.wait_ge(y_done, i + 1)
                nc.vector.tensor_tensor(core.x[:, bass.ds(i, 1), :], core.x[:, bass.ds(i, 1), :],
                                        yt[:, :].unsqueeze(1), ALU.add).then_inc(y_added, 1)

            def prepare_L1(i, rnd, k):
                def step(n):
                    dve.wait_ge(y_done, i * 5 + n)

                wait(dve, qk_full, i - 1)
                wait(dve, ready, 2 * i)
                nc.vector.tensor_scalar(yt[:, :].unsqueeze(1), core.x[:, bass.ds(i, 1), :], mv[:, bass.ds(i, 1), 0:1],
                                        factor[:, bass.ds(i, 1)], ALU.subtract, ALU.mult).then_inc(y_done, 1)
                step(1)
                nc.vector.tensor_tensor(yt[:, :], yt[:, :], w["qw"], ALU.mult).then_inc(y_done, 1)
                step(2)
                y3 = yt[:, :].rearrange("p (h a e) -> p h a e", h=H, a=2)
                r3 = rot[:, :].rearrange("p (h a e) -> p h a e", h=H, a=2)
                for a in range(2):
                    nc.vector.tensor_tensor(
                        r3[:, :, a, :], y3[:, :, 1 - a, :],
                        core.c("rope_sin")[:, a * 8:a * 8 + 8].unsqueeze(1).to_broadcast([P, H, 8]),
                        ALU.mult).then_inc(y_done, 1)
                step(4)
                nc.vector.tensor_tensor(
                    yt[:, :].rearrange("p (h e) -> p h e", h=H), yt[:, :].rearrange("p (h e) -> p h e", h=H),
                    core.c("rope_cos").unsqueeze(1).to_broadcast([P, H, E]), ALU.mult).then_inc(y_done, 1)
                step(5)
                nc.vector.tensor_tensor(zt[:, k, :, :].rearrange("p c q -> p (c q)"), yt[:, :], rot[:, :], ALU.add) \
                    .then_inc(ready, 1)
                nc.vector.tensor_scalar(
                    krow[:, k, :].rearrange("p (v g e) -> p v g e", v=KV, g=H // KV),
                    w["keys"][:, bass.ds(i, 1), :].rearrange("p t (v e) -> p (t v) e", v=KV).unsqueeze(2)
                    .to_broadcast([P, KV, H // KV, E]), 1.0, None, ALU.mult).then_inc(ready, 1)

            def spread_keys(i, rnd, k):
                dve.wait_ge(qk_full, i + 1)
                for c in range(NC):
                    last = nc.vector.tensor_tensor(
                        kbd[:, k, c, :, :, :],
                        qk_ps[:, D + c * P:D + (c + 1) * P].rearrange("p (b s) -> p b s", b=2).unsqueeze(2)
                        .to_broadcast([P, 2, 2, S]),
                        core.c("blk16").unsqueeze(1).unsqueeze(3).to_broadcast([P, 2, 2, S]), ALU.mult)
                last.then_inc(kbd_done, 1)

            def spread_values(i, rnd, k):
                if own:
                    dve.wait_ge(v_full, i + 1)
                else:
                    dve.wait_ge(v_in[k], (rnd + 1) * 32)
                for half in range(2):
                    rows = slice(half * S, (half + 1) * S)
                    if own:
                        src = v_ps[rows, :].rearrange("p (n h e) -> p n h e", h=2, e=E)[:, :, half, :]
                    else:
                        src = vrow[rows, k, :, :].rearrange("p b (v e) -> p (b v) e", e=E)
                    last = nc.vector.tensor_copy(
                        vbd[rows, k, :, :, half, :].rearrange("p b v e -> p (b v) e"), src)
                last.then_inc(vbd_done, 1)

            def shift(i, rnd, k):
                dve.wait_ge(s_full, i + 1)
                wait(dve, exped, i)
                nc.vector.tensor_tensor(
                    sc[:, :, :].rearrange("p (a h) s -> p a h s", a=4),
                    s_ps[:, :, 0:4 * S].rearrange("p a (h s) -> p a h s", s=S),
                    core.c("mask_ffn" if own else "mask_L1").unsqueeze(1).unsqueeze(1).to_broadcast([P, 4, 4, S]),
                    ALU.min).then_inc(masked, 1)
                dve.wait_ge(masked, i + 1)
                nc.vector.tensor_reduce(mx[:, :], sc[:, :, :], AX_X, ALU.max).then_inc(maxed, 1)
                dve.wait_ge(maxed, i + 1)
                nc.vector.tensor_tensor(sc[:, :, :], sc[:, :, :], mx[:, :].unsqueeze(2).to_broadcast([P, H, S]),
                                        ALU.subtract).then_inc(shifted, 1)

            def denominators(i, rnd, k):
                dve.wait_ge(exped, i + 1)
                wait(dve, att_done, i - 1)
                nc.vector.tensor_reduce(sm[:, :], ex[:, k, :, :], AX_X, ALU.add).then_inc(summed, 1)
                dve.wait_ge(summed, i + 1)
                nc.vector.reciprocal(rs[:, k, :], sm[:, :]).then_inc(inverted, 1)

            def attended(i, rnd, k):
                dve.wait_ge(o_full, i + 1)
                dve.wait_ge(inverted, i + 1)
                wait(dve, aT_full, i - 1)
                wait(dve, f_full, i - 1)
                for c in range(NC):
                    last = nc.vector.tensor_tensor(
                        att[:, k, c * P:(c + 1) * P].rearrange("p (j h e) -> p j h e", j=4, h=2),
                        o_ps[:, c * P:(c + 1) * P].rearrange("p (j h e) -> p j h e", j=4, h=2),
                        rs[:, k, :].rearrange("p (j c h) -> p j c h", j=4, c=2)[:, :, c, :].unsqueeze(3)
                        .to_broadcast([P, 4, 2, E]), ALU.mult)
                last.then_inc(att_done, 1)

            def finish(i, rnd, k):
                dve.wait_ge(f_full, i + 1)
                if own:
                    dve.wait_ge(tanhed, i + 1)
                    nc.vector.scalar_tensor_tensor(
                        out=mT[0:R, bass.ds(i, 1), :], in0=f_ps[0:R, P:2 * P].unsqueeze(1), scalar=0.1,
                        in1=th[:, :].unsqueeze(1), op0=ALU.mult, op1=ALU.mult).then_inc(f_out, 1)
                else:
                    nc.vector.tensor_tensor(core.x[:, bass.ds(i, 1), :], core.x[:, bass.ds(i, 1), :],
                                            f_ps.unsqueeze(1), ALU.add).then_inc(f_out, 1)

            run_steps(dve, NT, [(attended, 4), (spread_values, 2), (prepare_own if own else prepare_L1, 0),
                                (spread_keys, 1), (denominators, 3), (finish, 6), (shift, 2)])

        @block.scalar
        def _(act):
            def q_copy(i, rnd, k):
                act.wait_ge(qk_full, i + 1)
                wait(act, s_full, i - 1)
                act.wait_ge(kbd_done, i + 1)
                nc.scalar.activation(qT[:, k, :, :], qk_ps[:, 0:D].rearrange("p (c q) -> p c q", c=NC), ACT.Copy) \
                    .then_inc(q_out, 1)

            def exponent(i, rnd, k):
                act.wait_ge(shifted, i + 1)
                wait(act, pT_full, 2 * (i - 1))
                wait(act, summed, i - 1)
                nc.scalar.activation(ex[:, k, :, :], sc[:, :, :], ACT.Exp, scale=0.25).then_inc(exped, 1)

            def probT_copy(half):
                def part(i, rnd, k):
                    act.wait_ge(pT_full, 2 * i + half + 1)
                    nc.scalar.activation(probT[:, half, :, :], pT_ps[:, :].rearrange("p (b q) -> p b q", q=P),
                                         ACT.Copy).then_inc(pT_out, 1)
                return part

            def attT_copy(i, rnd, k):
                act.wait_ge(aT_full, i + 1)
                nc.scalar.activation(attT[:, :, :], f_ps.rearrange("p (c q) -> p c q", c=NC), ACT.Copy) \
                    .then_inc(aT_out, 1)

            def tanh(i, rnd, k):
                act.wait_ge(f_full, i + 1)
                wait(act, f_out, i)
                act.wait_ge(att_done, upto(i + 3))
                nc.scalar.activation(th[:, :], f_ps[0:R, 0:P], ACT.Tanh).then_inc(tanhed, 1)

            run_steps(act, NT, ([(tanh, 6)] if own else []) +
                      [(probT_copy(0), 3), (q_copy, 1), (probT_copy(1), 3), (attT_copy, 5), (exponent, 2)])

        @block.tensor
        def _(pe):
            def project(i, rnd, k):
                pe.wait_ge(ready, i + 1)
                wait(pe, q_out, i)
                wait(pe, kbd_done, i)
                for m, wt in enumerate((w["wq"], w["wk"])):
                    for co in range(NC):
                        for c in range(NC):
                            last = nc.tensor.matmul(qk_ps[:, m * D + co * P:m * D + (co + 1) * P],
                                                    wt[:, c, co * P:(co + 1) * P], zt[:, k, c, :],
                                                    start=(c == 0), stop=(c == NC - 1))
                last.then_inc(qk_full, 1)
                wait(pe, vbd_done, i)
                for b in range(2):
                    for half in range(2):
                        for c in range(NC):
                            last = nc.tensor.matmul(v_ps[half * S:(half + 1) * S, b * D:(b + 1) * D],
                                                    zt[:, k, c, b * S:(b + 1) * S], w["wv"][:, c, :],
                                                    start=(c == 0), stop=(c == NC - 1))
                last.then_inc(v_full, 1)

            def turn_qk(i, rnd, k):
                pe.wait_ge(ready, 2 * i + 2)
                wait(pe, q_out, i)
                wait(pe, kbd_done, i)
                for c in range(NC):
                    nc.tensor.transpose(qk_ps[:, c * P:(c + 1) * P], zt[:, k, c, :], core.c("ident"))
                for c in range(NC):
                    last = nc.tensor.transpose(qk_ps[:, D + c * P:D + (c + 1) * P], krow[:, k, c * P:(c + 1) * P],
                                               core.c("ident"))
                last.then_inc(qk_full, 1)

            def scores(i, rnd, k):
                pe.wait_ge(q_out, i + 1)
                pe.wait_ge(kbd_done, i + 1)
                wait(pe, masked, i)
                for j in range(4):
                    rows = slice(32 * j, 32 * j + 32)
                    for b in range(2):
                        for c in range(NC):
                            at = c * 2 * S
                            last = nc.tensor.matmul(
                                s_ps[b * S:(b + 1) * S, j, at:at + 2 * S], qT[rows, k, c, b * S:(b + 1) * S],
                                kbd[rows, k, c, b, :, :].rearrange("p h s -> p (h s)"), start=True, stop=True)
                last.then_inc(s_full, 1)

            def turn(half):
                def part(i, rnd, k):
                    pe.wait_ge(exped, i + 1)
                    wait(pe, pT_out, 2 * i + half)
                    for m in range(PAIRS // 2):
                        n = half * PAIRS // 2 + m
                        last = nc.tensor.transpose(pT_ps[:, m * P:(m + 1) * P],
                                                   ex[:, k, 2 * n:2 * n + 2, :].rearrange("p h s -> p (h s)"),
                                                   core.c("ident"))
                    last.then_inc(pT_full, 1)
                return part

            def weigh(half):
                def part(i, rnd, k):
                    if half == 0:
                        wait(pe, att_done, i)
                        wait(pe, aT_out, i - 1)
                        wait(pe, f_out, i - 2)
                        pe.wait_ge(vbd_done, i + 1)
                    pe.wait_ge(pT_out, 2 * i + half + 1)
                    for m in range(PAIRS // 2):
                        n = half * PAIRS // 2 + m
                        j, c = n // 2, n % 2
                        pair = c * 4 + j
                        for b in range(2):
                            last = nc.tensor.matmul(
                                o_ps[b * S:(b + 1) * S, pair * 2 * E:(pair + 1) * 2 * E],
                                probT[:, half, m, b * S:(b + 1) * S],
                                vbd[:, k, b, pair if own else pair // 2, :, :].rearrange("p h e -> p (h e)"),
                                start=True, stop=True)
                    if half:
                        last.then_inc(o_full, 1)
                return part

            def turn_att(i, rnd, k):
                pe.wait_ge(att_done, upto(i + 2))
                wait(pe, f_out, i)
                for c in range(NC):
                    last = nc.tensor.transpose(f_ps[:, c * P:(c + 1) * P], att[:, k, c * P:(c + 1) * P],
                                               core.c("ident"))
                last.then_inc(aT_full, 1)

            def final(i, rnd, k):
                pe.wait_ge(aT_out, i + 1)
                if own:
                    for c in range(NC):
                        nc.tensor.matmul(f_ps[0:R, 0:P], w["WoA"][:, c, :], attT[:, c, :],
                                         start=(c == 0), stop=(c == NC - 1))
                    for c in range(NC):
                        last = nc.tensor.matmul(f_ps[0:R, P:2 * P], w["A2"][:, c, :],
                                                zT[:, c:c + 1, bass.ds(i, 1), :].rearrange("p c t q -> p (c t) q"),
                                                start=(c == 0), stop=(c == NC - 1))
                else:
                    for c in range(NC):
                        last = nc.tensor.matmul(f_ps[:, :], attT[:, c, :], w["wo"][:, c, :],
                                                start=(c == 0), stop=(c == NC - 1))
                last.then_inc(f_full, 1)

            run_steps(pe, NT, [(turn(0), 3), (project if own else turn_qk, 1), (turn(1), 3), (scores, 2),
                               (turn_att, 5), (weigh(0), 3), (weigh(1), 3), (final, 5)])


def feed_forward(core, tag, zT, gate_w, up_w, down_w, F, kind, mod=None):
    nc = core.nc
    FC = F // P
    G = 4
    TG = NT // G
    U = G * FC
    with ExitStack() as ctx:
        room = Room(nc, ctx, tag)
        act_sb = room.sb("act_sb", [P, 2, 512])
        hid = room.sb("hid", [P, 2, 512])
        g_ps = room.ps("g_ps", [P, 2, 512])
        u_ps = room.ps("u_ps", [P, 2, 512])
        o_ps = room.ps("o_ps", [P, TG, 512])
        g_full, u_full, acted, hid_done, used, o_full, o_out = room.sems(
            "g_full", "u_full", "acted", "hid_done", "used", "o_full", "o_out")
        block = ctx.enter_context(nc.Block())

        @block.tensor
        def _(pe):
            def gate_up(u, rnd, f):
                s = f % 2
                wait(pe, acted, u - 1)
                wait(pe, hid_done, u - 1)
                for ps, wt, full in ((g_ps, gate_w, g_full), (u_ps, up_w, u_full)):
                    last_c = NC - 1
                    for c in range(NC):
                        last = nc.tensor.matmul(ps[:, s, :], wt[:, c, f * P:(f + 1) * P],
                                                zT[:, c:c + 1, bass.ds(rnd * TG, TG), :]
                                                .rearrange("p c t q -> p (c t) q"),
                                                start=(c == 0), stop=(c == last_c and not (mod and ps is g_ps)))
                    if mod and ps is g_ps:
                        mT, Bw = mod
                        last = nc.tensor.matmul(ps[:, s, :], Bw[:, f * P:(f + 1) * P],
                                                mT[:, bass.ds(rnd * TG, TG), :], start=False, stop=True)
                    last.then_inc(full, 1)

            def down(u, rnd, f):
                pe.wait_ge(hid_done, u + 1)
                if f == 0:
                    wait(pe, o_out, rnd)
                for t in range(TG):
                    last = nc.tensor.matmul(o_ps[:, t, 0:D], hid[:, f % 2, t * P:(t + 1) * P], down_w[:, f, :],
                                            start=(f == 0), stop=(f == FC - 1))
                last.then_inc(used, 1)

            run_steps(pe, U, [(gate_up, 0), (down, 1)], unroll=FC)

        @block.scalar
        def _(act):
            def activate(u, rnd, f):
                act.wait_ge(g_full, u + 1)
                wait(act, hid_done, u - 1)
                nc.scalar.activation(act_sb[:, f % 2, :], g_ps[:, f % 2, :], kind).then_inc(acted, 1)

            run_steps(act, U, [(activate, 0)], unroll=FC)

        @block.vector
        def _(dve):
            def multiply(u, rnd, f):
                dve.wait_ge(u_full, u + 1)
                dve.wait_ge(acted, u + 1)
                wait(dve, used, u - 1)
                nc.vector.tensor_tensor(hid[:, f % 2, :], act_sb[:, f % 2, :], u_ps[:, f % 2, :], ALU.mult) \
                    .then_inc(hid_done, 1)

            def add(u, rnd, f):
                if f != FC - 1:
                    return
                dve.wait_ge(used, u + 1)
                nc.vector.tensor_tensor(core.x[:, bass.ds(rnd * TG, TG), :], core.x[:, bass.ds(rnd * TG, TG), :],
                                        o_ps[:, :, 0:D], ALU.add).then_inc(o_out, 1)

            run_steps(dve, U, [(multiply, 0), (add, 1)], unroll=FC)


def stage_L0_ffn(core):
    nc, ins = core.nc, core.ins
    F, R = 1024, 16
    with ExitStack() as ctx:
        room = Room(nc, ctx, "s3")
        mv = room.sb("mv", [P, NT, 2])
        rstd = room.sb("rstd", [P, NT])
        factor = room.sb("factor", [P, NT])
        zT = room.sb("zT", [P, NC, NT, P])
        mT = room.sb("mT", [R, NT, P])
        w = {n: room.sb(n, [P, NC, D]) for n in ("wq", "wk", "wv", "wo")}
        w["A"] = room.sb("A", [P, NC, R])
        w["A2"] = room.sb("A2", [P, NC, R])
        w["WoA"] = room.sb("WoA", [P, NC, R])
        w["in"] = room.sb("in", [P, NC, F])
        w["up"] = room.sb("up", [P, NC, F])
        w["down"] = room.sb("down", [P, F // P, D])
        w["B"] = room.sb("B", [R, F])
        ln = room.sb("ln", [P, 2, NC])
        token_stats(core, mv, rstd, "s3n", "eps_rms", factor)
        turn_tokens(core, zT, mv, factor, "s3t")
        with ExitStack() as sctx:
            sroom = Room(nc, sctx, "s3w")
            wa_ps = sroom.ps("wa_ps", [P, NC, 512])
            w_in, wa_full, folded = sroom.sems("w_in", "wa_full", "folded")
            block = sctx.enter_context(nc.Block())
            loads = (("wq", "WqT"), ("wk", "WkT"), ("wv", "WvT"), ("wo", "L0_ffn_Wo"), ("A", "L0_ffn_A"),
                     ("in", "WinT"), ("up", "WupT"), ("down", "WdownT"))

            @block.sync
            def _(sp):
                for dst, src in loads:
                    sp.dma_start(w[dst][:, :, :], ins[src].rearrange("(c p) n -> p c n", p=P)).then_inc(w_in, 16)
                sp.dma_start(w["B"][:, :], ins["L0_ffn_B"]).then_inc(w_in, 16)
                sp.dma_start(ln[:, :, :], ins["ln_ffn"].rearrange("a (c p) -> p a c", p=P),
                             allow_slow_non_contiguous=True).then_inc(w_in, 16)

            @block.tensor
            def _(pe):
                pe.wait_ge(w_in, 16 * (len(loads) + 2))
                for ci in range(NC):
                    for co in range(NC):
                        last = nc.tensor.matmul(wa_ps[:, ci, 0:R], w["wo"][:, co, ci * P:(ci + 1) * P],
                                                w["A"][:, co, :], start=(co == 0), stop=(co == NC - 1))
                last.then_inc(wa_full, 1)

            @block.vector
            def _(dve):
                dve.wait_ge(w_in, 16 * (len(loads) + 2))
                for names, norm in ((("wq", "wk", "wv"), 0), (("in", "up"), 1)):
                    for n in names:
                        for c in range(NC):
                            nc.vector.tensor_scalar(w[n][:, c, :], w[n][:, c, :], ln[:, norm, c:c + 1], None, ALU.mult)
                for c in range(NC):
                    nc.vector.tensor_scalar(w["A2"][:, c, :], w["A"][:, c, :], ln[:, 1, c:c + 1], None, ALU.mult)
                dve.wait_ge(wa_full, 1)
                nc.vector.tensor_copy(w["WoA"][:, :, :], wa_ps[:, :, 0:R]).then_inc(folded, 1)

        attention16(core, "ffn", "s3a", mv, rstd, factor, w, zT, mT)
        feed_forward(core, "s3f", zT, w["in"], w["up"], w["down"], F, ACT.Silu, (mT, w["B"]))


def stage_L1_attention(core):
    nc, ins = core.nc, core.ins
    K, KQ, M, H = 32, 4, 8, 8
    MEM = K * H
    TAPS = 4
    QW = KQ * H * M * 2
    GROUPS, TG = 4, NT // 4
    BG = TG * 2
    Y = 48
    HK = K // 2
    N = HK * H * M
    UNITS = 2 * NT
    ROUND = 12582912.0
    TWO_PI = 6.2831845
    with ExitStack() as octx:
        oroom = Room(nc, octx, "s4")
        mv = oroom.sb("mv", [P, NT, 2])
        rstd = oroom.sb("rstd", [P, NT])
        kv_rows = oroom.sb("kv_rows", [P, NT, MEM])
        p_rows = oroom.sb("p_rows", [P, NT, K])
        inv_den = oroom.sb("inv_den", [P, NT, K])
        q_rows = oroom.sb("q_rows", [P, NT, QW])
        token_stats(core, mv, rstd, "s4n")

        with ExitStack() as ctx:
            room = Room(nc, ctx, "s4a")
            xT = room.sb("xT", [P, NC, NT, P])
            turn_tokens(core, xT, mv, rstd, "s4t")
            w_mem = room.sb("w_mem", [P, NC, MEM + K])
            w_q = room.sb("w_q", [P, NC, QW])
            taps = room.sb("taps", [P, 3, TAPS])
            small = room.sb("small", [K, 12])
            log_w = room.sb("log_w", [K, 512])
            zc = room.sb("zc", [P, 3, BG, S])
            pT = room.sb("pT", [K, 512])
            den = room.sb("den", [P, NT, K])
            z_ps = room.ps("z_ps", [P, 3, 512])
            r_ps = room.ps("r_ps", [P, 2, 512])
            q_ps = room.ps("q_ps", [P, 2, 512])
            d_ps = room.ps("d_ps", [P, 512])
            (w_in, z_full, z_link, conved, expT, r_full, r_out, q_full, q_out, d_full, sp_act, sp_dve,
             den_done) = room.sems(
                "w_in", "z_full", "z_link", "conved", "expT", "r_full", "r_out", "q_full", "q_out", "d_full",
                "sp_act", "sp_dve", "den_done")
            LOADS = 16 * 5
            block = ctx.enter_context(nc.Block())
            x_in, ab, e, u1, lnu, t, ri, prod, mx0, slope, neg, scl = (small[:, n:n + 1] for n in range(12))

            @block.sync
            def _(sp):
                sp.dma_start(w_mem[:, :, :], ins["L1_attn_W_mem"].rearrange("(c p) n -> p c n", p=P)) \
                    .then_inc(w_in, 16)
                sp.dma_start(w_q[:, :, :], ins["L1_attn_W_q"].rearrange("(c p) n -> p c n", p=P)).then_inc(w_in, 16)
                sp.dma_start(taps[:, :, :], ins["taps"].rearrange("(c p) w -> p c w", p=P)).then_inc(w_in, 16)
                sp.dma_start(x_in, ins["slopes"].rearrange("(p a) -> p a", a=1)).then_inc(w_in, 16)
                sp.dma_start(scl, ins["L1_attn_score_scale"].rearrange("(p a) -> p a", a=1)).then_inc(w_in, 16)

            @block.tensor
            def _(pe):
                pe.wait_ge(w_in, LOADS)
                for g in range(GROUPS):
                    wait(pe, conved, 4 * g)
                    for ch, m in enumerate((P, P, K)):
                        for c in range(NC):
                            last = nc.tensor.matmul(z_ps[0:m, ch, :], w_mem[:, c, ch * P:ch * P + m],
                                                    xT[:, c, g * TG:(g + 1) * TG, :],
                                                    start=(c == 0), stop=(c == NC - 1))
                        last.then_inc(z_full, 1)
                    for t_ in range(TG):
                        i = g * TG + t_
                        wait(pe, q_out, i - 1)
                        for c in range(NC):
                            last = nc.tensor.matmul(q_ps[:, i % 2, :], xT[:, c, i, :], w_q[:, c, :],
                                                    start=(c == 0), stop=(c == NC - 1))
                        last.then_inc(q_full, 1)
                    pe.wait_ge(conved, 4 * (g + 1))
                    pe.wait_ge(expT, g + 1)
                    for t_ in range(TG):
                        i = g * TG + t_
                        wait(pe, r_out, i - 1)
                        for ch in range(2):
                            nc.tensor.transpose(r_ps[:, i % 2, ch * P:(ch + 1) * P],
                                                zc[:, ch, 2 * t_:2 * t_ + 2, :].rearrange("p b s -> p (b s)"),
                                                core.c("ident"))
                        nc.tensor.transpose(r_ps[:, i % 2, MEM:MEM + K], pT[:, t_ * P:(t_ + 1) * P],
                                            core.c("ident", K)[:, 0:K]).then_inc(r_full, 1)
                pe.wait_ge(r_out, NT)
                for i in range(NT):
                    last = nc.tensor.matmul(d_ps[:, i * K:(i + 1) * K], core.c("tri"), p_rows[:, i, :],
                                            start=True, stop=True)
                last.then_inc(d_full, 1)

            @block.vector
            def _(dve):
                dve.wait_ge(w_in, LOADS)
                nc.vector.tensor_scalar(ab, x_in, -1.0, None, ALU.mult).then_inc(sp_dve, 1)
                dve.wait_ge(sp_dve, 1)
                nc.vector.tensor_tensor(ab, ab, x_in, ALU.min).then_inc(sp_dve, 1)
                dve.wait_ge(sp_act, 1)
                nc.vector.tensor_scalar(u1, e, 1.0, None, ALU.add).then_inc(sp_dve, 1)
                dve.wait_ge(sp_dve, 3)
                nc.vector.tensor_scalar(t, u1, 1.0, 1e-30, ALU.subtract, ALU.max).then_inc(sp_dve, 1)
                dve.wait_ge(sp_dve, 4)
                nc.vector.reciprocal(ri, t).then_inc(sp_dve, 1)
                nc.vector.tensor_scalar(mx0, x_in, 0.0, None, ALU.max).then_inc(sp_dve, 1)
                dve.wait_ge(sp_dve, 6)
                nc.vector.tensor_tensor(prod, e, ri, ALU.mult).then_inc(sp_dve, 1)
                dve.wait_ge(sp_dve, 7)
                dve.wait_ge(sp_act, 2)
                nc.vector.tensor_tensor(neg, prod, lnu, ALU.mult).then_inc(sp_dve, 1)
                dve.wait_ge(sp_dve, 8)
                nc.vector.tensor_tensor(slope, neg, mx0, ALU.add).then_inc(sp_dve, 1)
                dve.wait_ge(sp_dve, 9)
                nc.vector.tensor_scalar(log_w[:, :], core.c("age", K), slope, None, ALU.mult).then_inc(sp_dve, 1)
                dve.wait_ge(sp_dve, 10)
                step = [0]

                def link(ins_):
                    step[0] += 1
                    ins_.then_inc(z_link, 1)
                    dve.wait_ge(z_link, step[0])

                for g in range(GROUPS):
                    wait(dve, r_full, TG * g)
                    for ch, m in enumerate((P, P, K)):
                        dve.wait_ge(z_full, 3 * g + ch + 1)
                        z = z_ps[0:m, ch, :].rearrange("p (b s) -> p b s", s=S)
                        y = zc[0:m, ch, :, :]
                        link(nc.vector.tensor_scalar(y, z, taps[0:m, ch, 3:4], None, ALU.mult))
                        for back in (1, 2, 3):
                            ins_ = nc.vector.scalar_tensor_tensor(
                                out=y[:, :, back:S], in0=z[:, :, 0:S - back], scalar=taps[0:m, ch, 3 - back:4 - back],
                                in1=y[:, :, back:S], op0=ALU.mult, op1=ALU.add)
                            if back < 3:
                                link(ins_)
                        ins_.then_inc(conved, 1)
                    dve.wait_ge(conved, 4 * g + 3)
                    y = zc[0:K, 2, :, :].rearrange("p b s -> p (b s)")
                    link(nc.vector.tensor_scalar(y, y, scl, -20.0, ALU.mult, ALU.max))
                    nc.vector.scalar_tensor_tensor(out=y, in0=y, scalar=20.0, in1=log_w[:, :], op0=ALU.min,
                                                   op1=ALU.add).then_inc(conved, 1)
                dve.wait_ge(d_full, 1)
                nc.vector.tensor_scalar(den[:, :, :], d_ps[:, :].rearrange("p (t k) -> p t k", k=K), 1e-4, None,
                                        ALU.max).then_inc(den_done, 1)
                dve.wait_ge(den_done, 1)
                nc.vector.reciprocal(inv_den[:, :, :], den[:, :, :]).then_inc(den_done, 1)

            @block.scalar
            def _(act):
                act.wait_ge(sp_dve, 2)
                nc.scalar.activation(e, ab, ACT.Exp).then_inc(sp_act, 1)
                act.wait_ge(sp_dve, 3)
                nc.scalar.activation(lnu, u1, ACT.Ln).then_inc(sp_act, 1)
                for g in range(GROUPS):
                    for t_ in range(TG):
                        i = g * TG + t_
                        act.wait_ge(q_full, i + 1)
                        nc.scalar.activation(q_rows[:, i, :], q_ps[:, i % 2, :], ACT.Copy).then_inc(q_out, 1)
                    act.wait_ge(conved, 4 * (g + 1))
                    wait(act, r_full, TG * g)
                    nc.scalar.activation(pT[:, :], zc[0:K, 2, :, :].rearrange("p b s -> p (b s)"), ACT.Exp) \
                        .then_inc(expT, 1)
                    for t_ in range(TG):
                        i = g * TG + t_
                        act.wait_ge(r_full, i + 1)
                        nc.scalar.activation(kv_rows[:, i, :], r_ps[:, i % 2, 0:MEM], ACT.Copy)
                        nc.scalar.activation(p_rows[:, i, :], r_ps[:, i % 2, MEM:MEM + K], ACT.Copy).then_inc(r_out, 1)

        with ExitStack() as ctx:
            room = Room(nc, ctx, "s4b")
            theta = room.sb("theta", [P, 2, N])
            w_rows = room.sb("w_rows", [P, 2, 2, Y])
            norm = room.sb("norm", [P, 2])
            w_bd = room.sb("w_bd", [P, 2, 2, 2, HK, Y // 2])
            w_out = room.sb("w_out", [P, 6, D])
            turns = room.sb("turns", [P, N])
            whole = room.sb("whole", [P, N])
            frac = room.sb("frac", [P, 2, N])
            afrac = room.sb("afrac", [P, N])
            cs = room.sb("cs", [P, 2, 2, N])
            pcs = room.sb("pcs", [P, 2, 2, N])
            with_re = room.sb("with_re", [P, 2, 2, N])
            with_im = room.sb("with_im", [P, 2, 2, N])
            red = room.sb("red", [P, 2, HK * H])
            outs = room.sb("outs", [P, 2, 2, HK * H])
            outT = room.sb("outT", [P, 2, P])
            gate = room.sb("gate", [P, 2, HK * Y // 2])
            y = room.sb("y", [P, 2, HK * Y // 2])
            yT = room.sb("yT", [P, 2, 3, P])
            c_ps = room.ps("c_ps", [P, 2, N])
            y_ps = room.ps("y_ps", [P, 2, 512])
            t_ps = room.ps("t_ps", [P, 512])
            o_ps = room.ps("o_ps", [P, 512])
            (w_in, w_ready, turned, rounded, frac_done, abs_done, cs_done, pcs_done, c_full, prod_done, sum_done,
             red_done, outs_done, oT_full, oT_out, y_full, gated, y_done, yT_full, yT_out, o_full, added) = room.sems(
                "w_in", "w_ready", "turned", "rounded", "frac_done", "abs_done", "cs_done", "pcs_done", "c_full",
                "prod_done", "sum_done", "red_done", "outs_done", "oT_full", "oT_out", "y_full", "gated", "y_done",
                "yT_full", "yT_out", "o_full", "added")
            LOADS = 16 * 5
            block = ctx.enter_context(nc.Block())

            def upto(n, most):
                return min(n, most) if isinstance(n, int) else n

            @block.sync
            def _(sp):
                th = ins["L1_attn_theta"].rearrange("a b k h m -> (a b) (k h m)").to_broadcast([P, 2 * N])
                sp.dma_start(theta[:, :, :].rearrange("p a n -> p (a n)"), th).then_inc(w_in, 16)
                sp.dma_start(w_rows[:, :, 0, :], ins["L1_attn_W_re"].rearrange("(a k) h n -> (k h) a n", a=2)) \
                    .then_inc(w_in, 16)
                sp.dma_start(w_rows[:, :, 1, :], ins["L1_attn_W_im"].rearrange("(a k) h n -> (k h) a n", a=2)) \
                    .then_inc(w_in, 16)
                sp.dma_start(norm[:, :], ins["norm_T"]).then_inc(w_in, 16)
                sp.dma_start(w_out[:, :, :], ins["L1_attn_W_out"].rearrange("(c p) n -> p c n", p=P)) \
                    .then_inc(w_in, 16)

            def q_view(i, half, part):
                v = q_rows[:, bass.ds(i, 1), half * QW // 2:(half + 1) * QW // 2]
                v = v.rearrange("p t (g c two) -> p (t g) c two", g=2, two=2)[:, :, :, part]
                return v.unsqueeze(2).to_broadcast([P, 2, 8, H * M])

            @block.vector
            def _(dve):
                dve.wait_ge(w_in, LOADS)
                nc.vector.tensor_scalar(theta[:, :, :], theta[:, :, :], float(1 / (2 * np.pi)), None, ALU.mult) \
                    .then_inc(w_ready, 1)
                n = 1
                for half in range(2):
                    for part in range(2):
                        nc.vector.tensor_scalar(w_rows[:, half, part, :], w_rows[:, half, part, :],
                                                norm[:, half:half + 1], None, ALU.mult).then_inc(w_ready, 1)
                        n += 1
                dve.wait_ge(w_ready, n)
                for half in range(2):
                    for part in range(2):
                        for vg in range(2):
                            nc.vector.tensor_tensor(
                                w_bd[:, half, part, vg, :, :],
                                w_rows[:, half, part, vg * Y // 2:(vg + 1) * Y // 2].unsqueeze(1)
                                .to_broadcast([P, HK, Y // 2]),
                                core.c("blk_k").unsqueeze(2).to_broadcast([P, HK, Y // 2]), ALU.mult) \
                                .then_inc(w_ready, 1)
                            n += 1
                assert n == W_READY

                def fractions(u, i, half):
                    wait(dve, frac_done, u)
                    nc.vector.tensor_tensor(
                        turns[:, :].rearrange("p (a m) -> p a m", m=M),
                        kv_rows[:, bass.ds(i, 1), half * P:(half + 1) * P].rearrange("p t c -> p (t c)").unsqueeze(2)
                        .to_broadcast([P, P, M]),
                        theta[:, half, :].rearrange("p (a m) -> p a m", m=M), ALU.mult).then_inc(turned, 1)
                    dve.wait_ge(turned, u + 1)
                    nc.vector.tensor_scalar(whole[:, :], turns[:, :], ROUND, ROUND, ALU.add, ALU.subtract) \
                        .then_inc(rounded, 1)
                    dve.wait_ge(rounded, u + 1)
                    wait(dve, cs_done, 2 * (u - 1))
                    nc.vector.tensor_tensor(frac[:, half, :], turns[:, :], whole[:, :], ALU.subtract) \
                        .then_inc(frac_done, 1)

                def products(u, i, half):
                    dve.wait_ge(c_full, u + 1)
                    wait(dve, red_done, u - 1)
                    for part, dst in ((0, with_re), (1, with_im)):
                        for n_ in range(2):
                            src = c_ps[:, n_ if part == 0 else 1 - n_, :]
                            last = nc.vector.tensor_tensor(
                                dst[:, half, n_, :].rearrange("p (g k c) -> p g k c", g=2, k=8),
                                src.rearrange("p (g k c) -> p g k c", g=2, k=8), q_view(i, half, part), ALU.mult)
                    last.then_inc(prod_done, 1)

                def reduce(u, i, half):
                    dve.wait_ge(sum_done, 2 * (u + 1))
                    wait(dve, outs_done, u)
                    nc.vector.tensor_reduce(red[:, :, :], with_re[:, half, :, :].rearrange("p a (c m) -> p a c m", m=M),
                                            AX_X, ALU.add).then_inc(red_done, 1)
                    dve.wait_ge(red_done, u + 1)
                    wait(dve, oT_full, u - 1)
                    nc.vector.tensor_tensor(
                        outs[:, half, :, :].rearrange("p a (k h) -> p a k h", h=H),
                        red[:, :, :].rearrange("p a (k h) -> p a k h", h=H),
                        inv_den[:, bass.ds(i, 1), half * HK:(half + 1) * HK].unsqueeze(3).to_broadcast([P, 2, HK, H]),
                        ALU.mult).then_inc(outs_done, 1)

                def multiply(u, i, half):
                    dve.wait_ge(gated, u + 1)
                    wait(dve, yT_full, u - 1)
                    nc.vector.tensor_tensor(y[:, half, :], gate[:, half, :], y_ps[:, 0, 0:HK * Y // 2], ALU.mult) \
                        .then_inc(y_done, 1)

                def add(u, i, half):
                    if half == 0:
                        return
                    dve.wait_ge(o_full, i + 1)
                    nc.vector.tensor_tensor(core.x[:, bass.ds(i, 1), :], core.x[:, bass.ds(i, 1), :],
                                            o_ps[:, D:2 * D].unsqueeze(1), ALU.add).then_inc(added, 1)

                run_steps(dve, UNITS, [(multiply, 6), (reduce, 4), (fractions, 0), (add, 9), (products, 2)])

            @block.gpsimd
            def _(pool):
                def weight(u, i, half):
                    pool.wait_ge(cs_done, 2 * (u + 1))
                    wait(pool, c_full, u - 1)
                    for n_ in range(2):
                        last = nc.gpsimd.tensor_tensor(
                            pcs[:, half, n_, :].rearrange("p (k c) -> p k c", k=HK),
                            cs[:, half, n_, :].rearrange("p (k c) -> p k c", k=HK),
                            p_rows[:, bass.ds(i, 1), half * HK:(half + 1) * HK].rearrange("p t k -> p (t k)")
                            .unsqueeze(2).to_broadcast([P, HK, H * M]), ALU.mult)
                    last.then_inc(pcs_done, 1)

                def combine(u, i, half):
                    pool.wait_ge(prod_done, u + 1)
                    for n_, op in ((0, ALU.add), (1, ALU.subtract)):
                        nc.gpsimd.tensor_tensor(with_re[:, half, n_, :], with_re[:, half, n_, :],
                                                with_im[:, half, n_, :], op).then_inc(sum_done, 1)

                run_steps(pool, UNITS, [(weight, 1), (combine, 3)])

            @block.scalar
            def _(act):
                act.wait_ge(w_in, 16)

                def rotate(u, i, half):
                    act.wait_ge(frac_done, u + 1)
                    wait(act, pcs_done, u - 1)
                    nc.scalar.activation(cs[:, half, 1, :], frac[:, half, :], ACT.Sin, scale=TWO_PI) \
                        .then_inc(cs_done, 1)
                    wait(act, cs_done, 2 * u)
                    nc.scalar.activation(afrac[:, :], frac[:, half, :], ACT.Abs).then_inc(abs_done, 1)
                    act.wait_ge(abs_done, u + 1)
                    nc.scalar.activation(cs[:, half, 0, :], afrac[:, :], ACT.Sin, scale=-TWO_PI,
                                         bias=core.c("half_pi")).then_inc(cs_done, 1)

                def outT_copy(u, i, half):
                    act.wait_ge(oT_full, u + 1)
                    nc.scalar.activation(outT[:, :, :], o_ps[:, 0:2 * P].rearrange("p (a q) -> p a q", a=2), ACT.Copy) \
                        .then_inc(oT_out, 1)

                def gates(u, i, half):
                    act.wait_ge(y_full, u + 1)
                    wait(act, y_done, u - 1)
                    nc.scalar.activation(gate[:, half, :], y_ps[:, 1, 0:HK * Y // 2], ACT.Silu).then_inc(gated, 1)

                def yT_copy(u, i, half):
                    act.wait_ge(yT_full, u + 1)
                    wait(act, o_full, i)
                    nc.scalar.activation(yT[:, half, :, :], t_ps[:, 0:3 * P].rearrange("p (a q) -> p a q", a=3),
                                         ACT.Copy).then_inc(yT_out, 1)

                run_steps(act, UNITS, [(outT_copy, 5), (yT_copy, 7), (rotate, 0), (gates, 5)])

            @block.tensor
            def _(pe):
                pe.wait_ge(w_ready, W_READY)

                def running_sums(u, i, half):
                    pe.wait_ge(pcs_done, u + 1)
                    wait(pe, prod_done, u)
                    for n_ in range(2):
                        for b in range(N // 512):
                            last = nc.tensor.matmul(c_ps[:, n_, b * 512:(b + 1) * 512], core.c("tri"),
                                                    pcs[:, half, n_, b * 512:(b + 1) * 512], start=True, stop=True)
                    last.then_inc(c_full, 1)

                def turn_outs(u, i, half):
                    pe.wait_ge(outs_done, u + 1)
                    wait(pe, added, i - 2 + half)
                    for n_ in range(2):
                        last = nc.tensor.transpose(o_ps[:, n_ * P:(n_ + 1) * P], outs[:, half, n_, :], core.c("ident"))
                    last.then_inc(oT_full, 1)

                def heads(u, i, half):
                    pe.wait_ge(oT_out, u + 1)
                    wait(pe, y_done, u)
                    for vg in range(2):
                        for part in range(2):
                            last = nc.tensor.matmul(
                                y_ps[:, vg, 0:HK * Y // 2], outT[:, part, :],
                                w_bd[:, half, part, vg, :, :].rearrange("p k n -> p (k n)"),
                                start=(part == 0), stop=(part == 1))
                    last.then_inc(y_full, 1)

                def turn_y(u, i, half):
                    pe.wait_ge(y_done, u + 1)
                    wait(pe, yT_out, u)
                    for c in range(3):
                        last = nc.tensor.transpose(t_ps[:, c * P:(c + 1) * P], y[:, half, c * P:(c + 1) * P],
                                                   core.c("ident"))
                    last.then_inc(yT_full, 1)

                def output(u, i, half):
                    if half == 0:
                        return
                    pe.wait_ge(yT_out, u + 1)
                    wait(pe, added, i)
                    pe.wait_ge(oT_out, upto(u + 4, UNITS))
                    for c in range(6):
                        last = nc.tensor.matmul(o_ps[:, D:2 * D], yT[:, c // 3, c % 3, :], w_out[:, c, :],
                                                start=(c == 0), stop=(c == 5))
                    last.then_inc(o_full, 1)

                run_steps(pe, UNITS, [(running_sums, 2), (turn_outs, 5), (turn_y, 7), (heads, 5), (output, 8)])


W_READY = 13


def stage_L1_cross(core):
    nc, ins = core.nc, core.ins
    KV, E = 4, 16
    W = KV * E
    with ExitStack() as ctx:
        room = Room(nc, ctx, "s5")
        mv = room.sb("mv", [P, NT, 2])
        rstd = room.sb("rstd", [P, NT])
        factor = room.sb("factor", [P, NT])
        keys = room.sb("keys", [P, NT, W])
        qw = room.sb("qw", [P, D])
        wo = room.sb("wo", [P, NC, D])
        token_stats(core, mv, rstd, "s5n", "eps_rms5", factor)
        with ExitStack() as sctx:
            sroom = Room(nc, sctx, "s5k")
            raw = sroom.sb("raw", [P, NT, W])
            kn = sroom.sb("kn", [P, NT, W])
            rot = sroom.sb("rot", [P, NT, W])
            kw = sroom.sb("kw", [P, W])
            ss = sroom.sb("ss", [P, NT])
            root = sroom.sb("root", [P, NT])
            inv = sroom.sb("inv", [P, NT])
            loaded, step_done, rooted = sroom.sems("loaded", "step_done", "rooted")
            block = sctx.enter_context(nc.Block())

            @block.sync
            def _(sp):
                sp.dma_start(raw[:, :, :], ins["ctx_512"].rearrange("(t b) k d -> (b k) t d", b=2)) \
                    .then_inc(loaded, 16)
                sp.dma_start(kw[:, :], ins["L1_xattn_k_norm_w"].rearrange("(a n) -> a n", a=1).to_broadcast([P, W])) \
                    .then_inc(loaded, 16)
                sp.dma_start(qw[:, :], ins["L1_xattn_q_norm_w"].rearrange("(a n) -> a n", a=1).to_broadcast([P, D])) \
                    .then_inc(loaded, 16)
                sp.dma_start(wo[:, :, :], ins["L1_woT"].rearrange("(c p) n -> p c n", p=P)).then_inc(loaded, 16)
                sp.wait_ge(loaded, 64)

            @block.scalar
            def _(act):
                act.wait_ge(step_done, 2)
                nc.scalar.activation(root[:, :], ss[:, :], ACT.Sqrt, bias=core.c("eps_rms5"), scale=1.0 / W) \
                    .then_inc(rooted, 1)

            @block.vector
            def _(dve):
                dve.wait_ge(loaded, 64)
                nc.vector.tensor_tensor(kn[:, :, :], raw[:, :, :], raw[:, :, :], ALU.mult).then_inc(step_done, 1)
                dve.wait_ge(step_done, 1)
                nc.vector.tensor_reduce(ss[:, :], kn[:, :, :], AX_X, ALU.add).then_inc(step_done, 1)
                dve.wait_ge(rooted, 1)
                nc.vector.reciprocal(inv[:, :], root[:, :]).then_inc(step_done, 1)
                dve.wait_ge(step_done, 3)
                nc.vector.tensor_tensor(kn[:, :, :], raw[:, :, :], inv[:, :].unsqueeze(2).to_broadcast([P, NT, W]),
                                        ALU.mult).then_inc(step_done, 1)
                dve.wait_ge(step_done, 4)
                nc.vector.tensor_tensor(kn[:, :, :], kn[:, :, :], kw[:, :].unsqueeze(1).to_broadcast([P, NT, W]),
                                        ALU.mult).then_inc(step_done, 1)
                dve.wait_ge(step_done, 5)
                k3 = kn[:, :, :].rearrange("p t (v a e) -> p (t v) a e", v=KV, a=2)
                r3 = rot[:, :, :].rearrange("p t (v a e) -> p (t v) a e", v=KV, a=2)
                for a in range(2):
                    nc.vector.tensor_tensor(
                        r3[:, :, a, :], k3[:, :, 1 - a, :],
                        core.c("rope_sin")[:, a * 8:a * 8 + 8].unsqueeze(1).to_broadcast([P, NT * KV, 8]),
                        ALU.mult).then_inc(step_done, 1)
                dve.wait_ge(step_done, 7)
                kf = kn[:, :, :].rearrange("p t (v e) -> p (t v) e", v=KV)
                nc.vector.tensor_tensor(kf, kf, core.c("rope_cos").unsqueeze(1).to_broadcast([P, NT * KV, E]),
                                        ALU.mult).then_inc(step_done, 1)
                dve.wait_ge(step_done, 8)
                nc.vector.tensor_tensor(keys[:, :, :], kn[:, :, :], rot[:, :, :], ALU.add).then_inc(step_done, 1)

        attention16(core, "L1", "s5a", mv, rstd, factor, {"qw": qw[:, :], "keys": keys, "wo": wo})


def stage_L1_ffn(core):
    nc, ins = core.nc, core.ins
    F = 2048
    CHUNK = 1024
    with ExitStack() as ctx:
        room = Room(nc, ctx, "s6")
        mv = room.sb("mv", [P, NT, 2])
        rstd = room.sb("rstd", [P, NT])
        zT = room.sb("zT", [P, NC, NT, P])
        gate_w = room.sb("gate_w", [P, 2, F])
        up_w = room.sb("up_w", [P, 2, F])
        down_w = room.sb("down_w", [P, F // P, D])
        token_stats(core, mv, rstd, "s6n")
        turn_tokens(core, zT, mv, rstd, "s6t", column_step=2)
        with ExitStack() as sctx:
            sroom = Room(nc, sctx, "s6w")
            packed = sroom.sb("packed", [P, 2, CHUNK], I32)
            scale = sroom.sb("scale", [P, 2, CHUNK])
            code = sroom.sb("code", [P, CHUNK], I32)
            sign = sroom.sb("sign", [P, CHUNK], I32)
            over4 = sroom.sb("over4", [P, CHUNK])
            over6 = sroom.sb("over6", [P, CHUNK])
            half = sroom.sb("half", [P, CHUNK])
            over = sroom.sb("over", [P, CHUNK])
            size = sroom.sb("size", [P, CHUNK])
            value = sroom.sb("value", [P, CHUNK])
            in0, in1, made, step_done = sroom.sems("in0", "in1", "made", "step_done")
            chunk_in = (in0, in1)
            block = sctx.enter_context(nc.Block())
            chunks = []
            for m, w in (("gate", gate_w), ("up", up_w)):
                for a in range(F // CHUNK):
                    cols = slice(a * CHUNK, (a + 1) * CHUNK)
                    chunks.append((m, cols, [w[:, n, cols] for n in range(2)]))
            for a in range(F // CHUNK):
                cols = slice(a * CHUNK, (a + 1) * CHUNK)
                q = CHUNK // D
                v = down_w[:, :, :].rearrange("p (q two) h -> p q two h", two=2)
                chunks.append(("down", cols, [v[:, a * q:(a + 1) * q, n, :] for n in range(2)]))

            @block.sync
            def _(sp):
                for n, (m, cols, _) in enumerate(chunks):
                    if n >= 2:
                        sp.wait_ge(made, 2 * (n - 1))
                    sp.dma_start(packed[:, n % 2, :], ins[m + "_codes"][:, cols]).then_inc(chunk_in[n % 2], 16)
                    sp.dma_start(scale[:, n % 2, :], ins[m + "_scale_rows"][:, cols]).then_inc(chunk_in[n % 2], 16)

            @block.vector
            def _(dve):
                done = 0
                for n, (_, _, targets) in enumerate(chunks):
                    dve.wait_ge(chunk_in[n % 2], 32 * (n // 2 + 1))
                    for high, dst in enumerate(targets):
                        if done:
                            dve.wait_ge(step_done, done)
                            dve.wait_ge(made, 2 * n + high)
                        nc.vector.tensor_scalar(code[:, :], packed[:, n % 2, :], 4 * high, 7,
                                                ALU.logical_shift_right, ALU.bitwise_and).then_inc(step_done, 1)
                        nc.vector.tensor_scalar(sign[:, :], packed[:, n % 2, :], 4 * high, 8,
                                                ALU.logical_shift_right, ALU.bitwise_and).then_inc(step_done, 1)
                        dve.wait_ge(step_done, done + 2)
                        nc.vector.tensor_scalar(over4[:, :], code[:, :], 4.0, 0.0, ALU.subtract, ALU.max) \
                            .then_inc(step_done, 1)
                        nc.vector.tensor_scalar(over6[:, :], code[:, :], 6.0, 0.0, ALU.subtract, ALU.max) \
                            .then_inc(step_done, 1)
                        nc.vector.tensor_scalar(half[:, :], sign[:, :], -0.125, 0.5, ALU.mult, ALU.add) \
                            .then_inc(step_done, 1)
                        dve.wait_ge(step_done, done + 5)
                        nc.vector.scalar_tensor_tensor(out=over[:, :], in0=over6[:, :], scalar=2.0, in1=over4[:, :],
                                                       op0=ALU.mult, op1=ALU.add).then_inc(step_done, 1)
                        dve.wait_ge(step_done, done + 6)
                        nc.vector.tensor_tensor(size[:, :], code[:, :], over[:, :], ALU.add).then_inc(step_done, 1)
                        dve.wait_ge(step_done, done + 7)
                        nc.vector.tensor_tensor(value[:, :], size[:, :], half[:, :], ALU.mult).then_inc(step_done, 1)
                        done += 8
                        dve.wait_ge(step_done, done)
                        a, b = value[:, :], scale[:, n % 2, :]
                        if len(dst.shape) == 3:
                            a, b = (t.rearrange("p (q h) -> p q h", h=D) for t in (a, b))
                        nc.vector.tensor_tensor(dst, a, b, ALU.mult).then_inc(made, 1)

        feed_forward(core, "s6f", zT, gate_w, up_w, down_w, F, ACT.Gelu_apprx_tanh)


def columns_by_parity(a):
    return a.reshape(a.shape[0], 8, P, 2).transpose(0, 1, 3, 2).reshape(a.shape[0], -1)


LAYOUTS = {
    "bias_L0": lambda i: np.stack([i["L0_attn_b_Q"], i["L0_attn_b_K"], i["L0_attn_b_V"]], 2),
    "ctx_rep8": lambda i: np.repeat(i["ctx_512"].reshape(NT, P, 2, 4, 1, 8), 4, 4)
        .transpose(0, 3, 4, 5, 2, 1).reshape(NT, P, 2, P),
    "WqT": lambda i: i["L0_ffn_Wq"].T,
    "WkT": lambda i: i["L0_ffn_Wk"].T,
    "WvT": lambda i: i["L0_ffn_Wv"].T,
    "WinT": lambda i: i["L0_ffn_W_in_base"].T,
    "WupT": lambda i: i["L0_ffn_W_up_base"].T,
    "WdownT": lambda i: i["L0_ffn_W_down"].T,
    "taps": lambda i: np.pad(i["L1_attn_conv_k"][:, 0, :].T, ((0, 96), (0, 0))),
    "slopes": lambda i: np.concatenate([i["L1_attn_decay_slopes"], i["L1_attn_anchor_slopes"]]),
    "norm_T": lambda i: i["L1_attn_norm_scale"].reshape(2, P).T,
    "L1_woT": lambda i: i["L1_xattn_w_out"].T,
    "gate_codes": lambda i: columns_by_parity(i["L1_ffn_gate_W_packed"].T),
    "up_codes": lambda i: columns_by_parity(i["L1_ffn_up_W_packed"].T),
    "down_codes": lambda i: i["L1_ffn_down_W_packed"].T.reshape(8, P, D).transpose(1, 0, 2).reshape(P, 8 * D),
    "gate_scale_rows": lambda i: np.repeat(columns_by_parity(i["L1_ffn_gate_scales"].T), 16, 0),
    "up_scale_rows": lambda i: np.repeat(columns_by_parity(i["L1_ffn_up_scales"].T), 16, 0),
    "down_scale_rows": lambda i: np.repeat(i["L1_ffn_down_scales"].T.reshape(8, 8, 1, D), 16, 2)
        .reshape(8, P, D).transpose(1, 0, 2).reshape(P, 8 * D),
    "ln_ffn": lambda i: np.stack([i["L0_ffn_ln1_w"], i["L0_ffn_ln2_w"]]),
}
USED = {"x", "const", "bias_L0", "L0_attn_b_O", "L0_attn_W_Q", "L0_attn_W_K", "L0_attn_W_V",
        "L0_attn_W_O",
        "ctx_512", "ctx_rep8", "WqT", "WkT", "WvT", "WinT", "WupT", "WdownT", "L0_ffn_Wo", "L0_ffn_A",
        "L0_ffn_B", "ln_ffn", "L1_attn_W_mem", "L1_attn_W_q", "taps", "slopes", "norm_T",
        "L1_attn_score_scale", "L1_attn_theta", "L1_attn_W_re", "L1_attn_W_im", "L1_attn_W_out", "L1_woT",
        "L1_xattn_k_norm_w", "L1_xattn_q_norm_w", "gate_codes", "up_codes", "down_codes", "gate_scale_rows",
        "up_scale_rows", "down_scale_rows"}


def decoder(nc, ins, out):
    with ExitStack() as ctx:
        core = Core(nc, ctx, ins)
        run_stage(core, load)
        for n, stage in STAGE.items():
            if n in STAGES:
                run_stage(core, stage)
        run_stage(core, lambda core: store(core, out))


def load(core):
    with ExitStack() as ctx:
        (x_in,) = Room(core.nc, ctx, "ld").sems("x_in")
        block = ctx.enter_context(core.nc.Block())

        @block.sync
        def _(sp):
            sp.dma_start(core.x[:, :, :], core.ins["x"].rearrange("(t p) d -> p t d", p=P)).then_inc(x_in, 16)
            sp.dma_start(core.const[:, :], core.ins["const"]).then_inc(x_in, 16)
            sp.wait_ge(x_in, 32)


def store(core, out):
    with ExitStack() as ctx:
        (stored,) = Room(core.nc, ctx, "st").sems("stored")
        block = ctx.enter_context(core.nc.Block())

        @block.sync
        def _(sp):
            sp.dma_start(out.rearrange("(t p) d -> p t d", p=P), core.x[:, :, :]).then_inc(stored, 16)
            sp.wait_ge(stored, 16)


STAGE = {"1": stage_L0_attention, "2": stage_L0_cross, "3": stage_L0_ffn, "4": stage_L1_attention,
         "5": stage_L1_cross, "6": stage_L1_ffn}


def kernel(**inputs):
    import concourse.bacc as bacc
    from concourse.bass_utils import run_bass_kernel_spmd

    arrays = {}
    for name, a in inputs.items():
        a = np.ascontiguousarray(a)
        if name == "x":
            a = a.reshape(TOK, D)
        arrays[name] = a
    for name, a in LAYOUTS.items():
        arrays[name] = np.ascontiguousarray(a({k: np.asarray(v) for k, v in inputs.items()}))
    arrays["const"] = constants()
    nc = bacc.Bacc("TRN2", target_bir_lowering=False, num_devices=1)
    ins, given = {}, {}
    for name, a in arrays.items():
        if name in USED:
            ins[name] = nc.dram_tensor(f"in_{name}", a.shape, mybir.dt.from_np(a.dtype), kind="ExternalInput").ap()
            given[f"in_{name}"] = a
    out = nc.dram_tensor("out", (TOK, D), F32, kind="ExternalOutput").ap()
    decoder(nc, ins, out)
    r = run_bass_kernel_spmd(nc, [given], core_ids=[0])
    return r.results[0]["out"].reshape(B, S, D)
```
